# Optimizing a Trainium2 kernel written in Bass

```python
import numpy as np
import jax
import jax.numpy as jnp

def _softmax(x, axis=-1):
    return jax.nn.softmax(x, axis=axis)

def _gelu(x):
    return jax.nn.gelu(x, approximate=True)

def _silu(x):
    return jax.nn.silu(x)

def _sigmoid(x):
    return jax.nn.sigmoid(x)

def _layernorm(x, axis=-1, eps=1e-05):
    m = jnp.mean(x, axis=axis, keepdims=True)
    v = jnp.var(x, axis=axis, keepdims=True)
    return (x - m) / jnp.sqrt(v + eps)

def _scatter_add(tgt, idx, src, axis=0):
    return tgt.at[idx].add(src)

def _segment_sum(src, seg, n):
    return jax.ops.segment_sum(src, seg, n)
kernel_name = 'mk_gps_d2_gnn_r8_ede1a0'

def setup_inputs(seed: int=0):
    np.random.seed(seed)
    _w = jnp.asarray

    def _rec_inputs():
        import jax
        import jax.numpy as jnp
        _gk = jax.random.key(seed)
        x = -0.0005963 + 1.001 * jax.random.normal(jax.random.fold_in(_gk, 1), (384, 1024), jnp.float32)
        src = jax.random.randint(jax.random.fold_in(_gk, 2), (12288,), 0, 384, jnp.int32)
        dst = jnp.minimum((384 * jax.random.uniform(jax.random.fold_in(_gk, 3), (12288,)) ** 2.0).astype(jnp.int32), 3071)
        _o = jnp.argsort(dst, stable=True)
        src = src[_o]
        dst = dst[_o]
        edge_type_5 = jax.random.randint(jax.random.fold_in(_gk, 13), (12288,), 0, 5, jnp.int32)
        return (x, src, dst, edge_type_5)
    x, src, dst, edge_type_5 = _rec_inputs()

    def _L0_gnn_setup():
        import jax, jax.numpy as jnp
        import numpy as np
        N = 384
        E = 12288
        IN_F = 1024
        OUT_F = 1024
        H = 16
        D = OUT_F // H
        NUM_ETYPES = 4

        def _build_mask(edge_index, edge_type, edge_type_weights, dtype):
            src, dst = (edge_index[0], edge_index[1])
            w = jax.nn.softplus(edge_type_weights)
            mask = jnp.full((N, N), -jnp.inf, dtype=dtype)
            mask = mask.at[src, dst].set(w[edge_type - 1])
            diag = jnp.diagonal(mask)
            idx = jnp.arange(N)
            mask = mask.at[idx, idx].set(jnp.where(jnp.isneginf(diag), w[3], diag))
            return mask
        key = jax.random.key(seed)
        ks = jax.random.split(key, 20)
        p = lambda k, shape: jax.random.normal(k, shape, dtype=jnp.float32) * 0.02
        return {'x': jax.random.normal(ks[0], (N, IN_F), dtype=jnp.float32), 'edge_index': jax.random.randint(ks[1], (2, E), 0, N), 'edge_type': jax.random.randint(ks[2], (E,), 1, NUM_ETYPES + 1), 'edge_type_weights': jnp.ones((NUM_ETYPES,), jnp.float32) + 0.1 * jax.random.normal(ks[3], (NUM_ETYPES,), dtype=jnp.float32), 'wq': p(ks[4], (OUT_F, IN_F)), 'bq': p(ks[5], (OUT_F,)), 'wk': p(ks[6], (OUT_F, IN_F)), 'bk': p(ks[7], (OUT_F,)), 'wv': p(ks[8], (OUT_F, IN_F)), 'bv': p(ks[9], (OUT_F,)), 'wiq': p(ks[10], (OUT_F, OUT_F)), 'biq': p(ks[11], (OUT_F,)), 'wik': p(ks[12], (OUT_F, OUT_F)), 'bik': p(ks[13], (OUT_F,)), 'wiv': p(ks[14], (OUT_F, OUT_F)), 'biv': p(ks[15], (OUT_F,)), 'wo': p(ks[16], (OUT_F, OUT_F)), 'bo': p(ks[17], (OUT_F,))}
    _L0_gnn_all = _L0_gnn_setup()
    _L0_gnn_in = {k: v for k, v in _L0_gnn_all.items() if k in ('edge_type_weights', 'wq', 'bq', 'wk', 'bk', 'wv', 'bv', 'wiq', 'biq', 'wik', 'bik', 'wiv', 'biv', 'wo', 'bo')}
    del _L0_gnn_all

    def _L0_mix_setup():
        import jax, jax.numpy as jnp
        import numpy as np
        import math
        D_MODEL = 1024
        N_HEADS = 16
        D_HEAD = D_MODEL // N_HEADS
        SEQ = 256
        BATCH = 2
        key = jax.random.key(seed)
        ks = jax.random.split(key, 8)
        xav = math.sqrt(2.0 / (D_MODEL + D_MODEL))

        def lin(k):
            return jax.random.normal(k, (D_MODEL, D_MODEL), jnp.float32) * xav
        zeros = jnp.zeros((D_MODEL,), jnp.float32)
        return {'x': jax.random.normal(ks[0], (SEQ, BATCH, D_MODEL), jnp.float32), 'beta': jax.random.normal(ks[1], (N_HEADS,), jnp.float32) * 0.1, 'Wq': lin(ks[2]), 'bq': zeros, 'Wk': lin(ks[3]), 'bk': zeros, 'Wv': lin(ks[4]), 'bv': zeros, 'Wo': lin(ks[5]), 'bo': zeros}
    _L0_mix_all = _L0_mix_setup()
    _L0_mix_in = {k: v for k, v in _L0_mix_all.items() if k in ('beta', 'Wq', 'bq', 'Wk', 'bk', 'Wv', 'bv', 'Wo', 'bo')}
    del _L0_mix_all

    def _L0_ffn_setup():
        import jax, jax.numpy as jnp
        import numpy as np
        TOP_K = 2
        key = jax.random.key(seed)
        k1, k2, k3, k4 = jax.random.split(key, 4)
        B, S, H, F, E = (2, 256, 1024, 352, 8)
        hidden_states = jax.random.normal(k1, (B, S, H), dtype=jnp.float32)
        wqkv = jax.random.normal(k2, (3 * E, H), dtype=jnp.float32) * 0.02
        w1 = jax.random.normal(k3, (E, 2 * F, H), dtype=jnp.float32) * 0.02
        w2 = jax.random.normal(k4, (E, H, F), dtype=jnp.float32) * 0.02
        return {'hidden_states': hidden_states, 'wqkv': wqkv, 'w1': w1, 'w2': w2}
    _L0_ffn_all = _L0_ffn_setup()
    _L0_ffn_in = {k: v for k, v in _L0_ffn_all.items() if k in ('wqkv', 'w1', 'w2')}
    del _L0_ffn_all

    def _L1_gnn_setup():
        import jax, jax.numpy as jnp
        import numpy as np
        NEG_SLOPE = 0.1
        EPS = 1e-05
        key = jax.random.key(seed)
        k1, k2, k3, k4, k5 = jax.random.split(key, 5)
        N, E, DIN, DOUT = (1250, 20000, 1024, 1024)
        x = jax.random.normal(k1, (N, DIN), dtype=jnp.float32)
        W = jax.random.normal(k2, (DIN, DOUT), dtype=jnp.float32) * 0.02
        a = jax.random.normal(k3, (1, 2 * DOUT), dtype=jnp.float32) * 0.02
        src = jax.random.randint(k4, (E,), 0, N, dtype=jnp.int64)
        dst = jax.random.randint(k5, (E,), 0, N, dtype=jnp.int64)
        return {'x': x, 'W': W, 'a': a, 'src': src, 'dst': dst}
    _L1_gnn_all = _L1_gnn_setup()
    _L1_gnn_in = {k: v for k, v in _L1_gnn_all.items() if k in ('W', 'a')}
    del _L1_gnn_all

    def _L1_mix_setup():
        import jax, jax.numpy as jnp
        import numpy as np
        H, DK, DV = (16, 64, 64)
        LN_EPS = 1e-05
        key = jax.random.key(seed)
        ks = jax.random.split(key, 5)
        B, N, D = (4, 512, 1024)
        s = 1.0 / np.sqrt(D)
        return {'inputs': jax.random.normal(ks[0], (B, N, D), dtype=jnp.float32), 'W_Q': jax.random.normal(ks[1], (D, H * DK), dtype=jnp.float32) * s, 'W_K': jax.random.normal(ks[2], (D, H * DK), dtype=jnp.float32) * s, 'W_V': jax.random.normal(ks[3], (D, H * DV), dtype=jnp.float32) * s, 'W_fc': jax.random.normal(ks[4], (H * DV, D), dtype=jnp.float32) * s, 'gamma': jnp.ones((D,), dtype=jnp.float32), 'beta': jnp.zeros((D,), dtype=jnp.float32)}
    _L1_mix_all = _L1_mix_setup()
    _L1_mix_in = {k: v for k, v in _L1_mix_all.items() if k in ('W_Q', 'W_K', 'W_V', 'W_fc', 'gamma', 'beta')}
    del _L1_mix_all

    def _L1_ffn_setup():
        import jax, jax.numpy as jnp
        import numpy as np
        E = 8
        EPS = 1e-05
        key = jax.random.key(seed)
        ks = jax.random.split(key, 6)
        d, f = (1024, 512)
        B, S = (2, 1024)
        x = jax.random.normal(ks[0], (B, S, d), dtype=jnp.float32)
        c = jax.random.normal(ks[1], (d, E), dtype=jnp.float32)
        q, _ = jnp.linalg.qr(c)
        centroids = (0.1 * q.T).astype(jnp.float32)
        w1 = jax.random.normal(ks[2], (E, d, f), dtype=jnp.float32) / np.sqrt(d).astype(np.float32)
        b1 = jnp.zeros((E, f), dtype=jnp.float32)
        w2 = jax.random.normal(ks[3], (E, f, d), dtype=jnp.float32) * 0.02
        b2 = jnp.zeros((E, d), dtype=jnp.float32)
        gamma = jnp.ones((E, d), dtype=jnp.float32)
        beta = jnp.zeros((E, d), dtype=jnp.float32)
        return dict(x=x, centroids=centroids, w1=w1, b1=b1, w2=w2, b2=b2, gamma=gamma, beta=beta)
    _L1_ffn_all = _L1_ffn_setup()
    _L1_ffn_in = {k: v for k, v in _L1_ffn_all.items() if k in ('centroids', 'w1', 'b1', 'w2', 'b2', 'gamma', 'beta')}
    del _L1_ffn_all
    return {'x': x, 'src': src, 'dst': dst, 'edge_type_5': edge_type_5, 'L0_gnn_edge_type_weights': _L0_gnn_in['edge_type_weights'], 'L0_gnn_wq': _L0_gnn_in['wq'], 'L0_gnn_bq': _L0_gnn_in['bq'], 'L0_gnn_wk': _L0_gnn_in['wk'], 'L0_gnn_bk': _L0_gnn_in['bk'], 'L0_gnn_wv': _L0_gnn_in['wv'], 'L0_gnn_bv': _L0_gnn_in['bv'], 'L0_gnn_wiq': _L0_gnn_in['wiq'], 'L0_gnn_biq': _L0_gnn_in['biq'], 'L0_gnn_wik': _L0_gnn_in['wik'], 'L0_gnn_bik': _L0_gnn_in['bik'], 'L0_gnn_wiv': _L0_gnn_in['wiv'], 'L0_gnn_biv': _L0_gnn_in['biv'], 'L0_gnn_wo': _L0_gnn_in['wo'], 'L0_gnn_bo': _L0_gnn_in['bo'], 'L0_mix_beta': _L0_mix_in['beta'], 'L0_mix_Wq': _L0_mix_in['Wq'], 'L0_mix_bq': _L0_mix_in['bq'], 'L0_mix_Wk': _L0_mix_in['Wk'], 'L0_mix_bk': _L0_mix_in['bk'], 'L0_mix_Wv': _L0_mix_in['Wv'], 'L0_mix_bv': _L0_mix_in['bv'], 'L0_mix_Wo': _L0_mix_in['Wo'], 'L0_mix_bo': _L0_mix_in['bo'], 'L0_ffn_wqkv': _L0_ffn_in['wqkv'], 'L0_ffn_w1': _L0_ffn_in['w1'], 'L0_ffn_w2': _L0_ffn_in['w2'], 'L1_gnn_W': _L1_gnn_in['W'], 'L1_gnn_a': _L1_gnn_in['a'], 'L1_mix_W_Q': _L1_mix_in['W_Q'], 'L1_mix_W_K': _L1_mix_in['W_K'], 'L1_mix_W_V': _L1_mix_in['W_V'], 'L1_mix_W_fc': _L1_mix_in['W_fc'], 'L1_mix_gamma': _L1_mix_in['gamma'], 'L1_mix_beta': _L1_mix_in['beta'], 'L1_ffn_centroids': _L1_ffn_in['centroids'], 'L1_ffn_w1': _L1_ffn_in['w1'], 'L1_ffn_b1': _L1_ffn_in['b1'], 'L1_ffn_w2': _L1_ffn_in['w2'], 'L1_ffn_b2': _L1_ffn_in['b2'], 'L1_ffn_gamma': _L1_ffn_in['gamma'], 'L1_ffn_beta': _L1_ffn_in['beta']}

def reference(x, src, dst, edge_type_5, L0_gnn_edge_type_weights, L0_gnn_wq, L0_gnn_bq, L0_gnn_wk, L0_gnn_bk, L0_gnn_wv, L0_gnn_bv, L0_gnn_wiq, L0_gnn_biq, L0_gnn_wik, L0_gnn_bik, L0_gnn_wiv, L0_gnn_biv, L0_gnn_wo, L0_gnn_bo, L0_mix_beta, L0_mix_Wq, L0_mix_bq, L0_mix_Wk, L0_mix_bk, L0_mix_Wv, L0_mix_bv, L0_mix_Wo, L0_mix_bo, L0_ffn_wqkv, L0_ffn_w1, L0_ffn_w2, L1_gnn_W, L1_gnn_a, L1_mix_W_Q, L1_mix_W_K, L1_mix_W_V, L1_mix_W_fc, L1_mix_gamma, L1_mix_beta, L1_ffn_centroids, L1_ffn_w1, L1_ffn_b1, L1_ffn_w2, L1_ffn_b2, L1_ffn_gamma, L1_ffn_beta):
    import jax
    import jax.numpy as jnp

    def _L0_gnn_ref(x, edge_index, edge_type, edge_type_weights, wq, bq, wk, bk, wv, bv, wiq, biq, wik, bik, wiv, biv, wo, bo):
        import jax, jax.numpy as jnp
        import numpy as np
        N = 384
        E = 12288
        IN_F = 1024
        OUT_F = 1024
        H = 16
        D = OUT_F // H
        NUM_ETYPES = 4

        def _build_mask(edge_index, edge_type, edge_type_weights, dtype):
            src, dst = (edge_index[0], edge_index[1])
            w = jax.nn.softplus(edge_type_weights)
            mask = jnp.full((N, N), -jnp.inf, dtype=dtype)
            mask = mask.at[src, dst].set(w[edge_type - 1])
            diag = jnp.diagonal(mask)
            idx = jnp.arange(N)
            mask = mask.at[idx, idx].set(jnp.where(jnp.isneginf(diag), w[3], diag))
            return mask
        q = x @ wq.T + bq
        k = x @ wk.T + bk
        v = x @ wv.T + bv
        q2 = (q @ wiq.T + biq).reshape(N, H, D).transpose(1, 0, 2)
        k2 = (k @ wik.T + bik).reshape(N, H, D).transpose(1, 0, 2)
        v2 = (v @ wiv.T + biv).reshape(N, H, D).transpose(1, 0, 2)
        mask = _build_mask(edge_index, edge_type, edge_type_weights, x.dtype)
        scale = 1.0 / np.sqrt(D).astype(np.float32)
        scores = jnp.einsum('hnd,hmd->hnm', q2, k2) * scale + mask[None]
        attn = jax.nn.softmax(scores, axis=-1)
        out = jnp.einsum('hnm,hmd->hnd', attn, v2)
        out = out.transpose(1, 0, 2).reshape(N, OUT_F)
        return out @ wo.T + bo

    def _L0_mix_ref(x, beta, Wq, bq, Wk, bk, Wv, bv, Wo, bo):
        import jax, jax.numpy as jnp
        import numpy as np
        import math
        D_MODEL = 1024
        N_HEADS = 16
        D_HEAD = D_MODEL // N_HEADS
        SEQ = 256
        BATCH = 2
        s, b, d = x.shape
        h, dh = (N_HEADS, D_HEAD)

        def proj(W, bias):
            y = x @ W.T + bias
            return y.reshape(s, b, h, dh).transpose(1, 2, 0, 3)
        q = proj(Wq, bq)
        k = proj(Wk, bk)
        v = proj(Wv, bv)
        scale = math.sqrt(dh) * jnp.exp(beta)[None, :, None, None]
        q = jax.nn.softplus(q / scale)
        k = jax.nn.softplus(k / scale)
        kv = jnp.cumsum(k[..., :, None] * v[..., None, :], axis=2)
        kn = jnp.cumsum(k, axis=2)
        num = jnp.einsum('bhsk,bhskv->bhsv', q, kv)
        den = jnp.einsum('bhsk,bhsk->bhs', q, kn)
        out = num / den[..., None]
        out = out.transpose(2, 0, 1, 3).reshape(s, b, d)
        return out @ Wo.T + bo

    def _L0_ffn_ref(hidden_states, wqkv, w1, w2):
        import jax, jax.numpy as jnp
        import numpy as np
        TOP_K = 2
        b, s, h = hidden_states.shape
        E = w1.shape[0]
        mixed = hidden_states @ wqkv.T
        q, k, v = jnp.split(mixed, 3, axis=-1)
        q = q.astype(jnp.float32)
        k = k.astype(jnp.float32)
        v = v.astype(jnp.float32)
        attn = jax.nn.softmax(q[..., :, None] * k[..., None, :], axis=-1)
        logits = jnp.einsum('bsej,bsj->bse', attn, v).reshape(-1, E)
        top_logits, idx = jax.lax.top_k(logits, TOP_K)
        scores = jax.nn.softmax(top_logits.astype(jnp.float32), axis=-1).astype(hidden_states.dtype)
        N = b * s
        x = hidden_states.reshape(N, h)
        token_ids = jnp.repeat(jnp.arange(N), TOP_K)
        expert_ids = idx.reshape(-1)
        x_rep = x[token_ids]
        out = jnp.zeros_like(x_rep)
        for e in range(E):
            h1 = x_rep @ w1[e].T
            a, g = jnp.split(h1, 2, axis=-1)
            he = jax.nn.silu(a) * g @ w2[e].T
            out = out + jnp.where((expert_ids == e)[:, None], he, jnp.zeros((), out.dtype))
        out = out * scores.reshape(-1, 1)
        combined = out.reshape(N, TOP_K, h).sum(axis=1)
        return combined.reshape(b, s, h)

    def _L1_gnn_ref(x, W, a, src, dst):
        import jax, jax.numpy as jnp
        import numpy as np
        NEG_SLOPE = 0.1
        EPS = 1e-05
        N = x.shape[0]
        d = W.shape[1]
        h = x @ W
        a_l, a_r = (a[0, :d], a[0, d:])
        al = h @ a_l
        ar = h @ a_r
        e = jnp.exp(-jax.nn.leaky_relu(al[src] + ar[dst], negative_slope=NEG_SLOPE))
        rowsum = jax.ops.segment_sum(e, src, num_segments=N)
        h_prime = jax.ops.segment_sum(e[:, None] * h[dst], src, num_segments=N)
        h_prime = h_prime / (rowsum[:, None] + EPS)
        return jax.nn.elu(h_prime)

    def _L1_mix_ref(inputs, W_Q, W_K, W_V, W_fc, gamma, beta):
        import jax, jax.numpy as jnp
        import numpy as np
        H, DK, DV = (16, 64, 64)
        LN_EPS = 1e-05
        B, N, D = inputs.shape
        Q = jax.nn.sigmoid((inputs @ W_Q).reshape(B, N, H, DK))
        K = jax.nn.sigmoid((inputs @ W_K).reshape(B, N, H, DK))
        V = (inputs @ W_V).reshape(B, N, H, DV)
        KV = jnp.einsum('bnhk,bnhv->bhkv', K, V)
        num = jnp.einsum('bnhk,bhkv->bnhv', Q, KV)
        k_sum = K.sum(axis=1)
        den = jnp.einsum('bnhk,bhk->bnh', Q, k_sum)[..., None] + 1e-08
        out = (num / den).reshape(B, N, H * DV) @ W_fc
        x = out + inputs
        mu = x.mean(axis=-1, keepdims=True)
        var = jnp.mean((x - mu) ** 2, axis=-1, keepdims=True)
        return (x - mu) * jax.lax.rsqrt(var + LN_EPS) * gamma + beta

    def _L1_ffn_ref(x, centroids, w1, b1, w2, b2, gamma, beta):
        import jax, jax.numpy as jnp
        import numpy as np
        E = 8
        EPS = 1e-05
        B, S, d = x.shape
        feats = x.reshape(-1, d)
        aff = feats @ centroids.T
        eid = jnp.argmax(aff, axis=1)
        mu = jnp.mean(feats, axis=-1, keepdims=True)
        var = jnp.var(feats, axis=-1, keepdims=True)
        xhat = (feats - mu) * jax.lax.rsqrt(var + EPS)
        out = jnp.zeros_like(feats)
        for e in range(E):
            mask = (eid == e).astype(feats.dtype)[:, None]
            h = xhat * gamma[e] + beta[e]
            y = feats + jax.nn.relu(h @ w1[e] + b1[e]) @ w2[e] + b2[e]
            alpha = jax.nn.sigmoid(feats @ centroids[e])[:, None]
            out = out + mask * (alpha * y + (1.0 - alpha) * feats)
        return out.reshape(B, S, d)
    edge_index = jnp.stack([src, dst])
    xn = _layernorm(x, axis=-1)
    x = x + _L0_gnn_ref(xn, edge_index, edge_type_5, L0_gnn_edge_type_weights, L0_gnn_wq, L0_gnn_bq, L0_gnn_wk, L0_gnn_bk, L0_gnn_wv, L0_gnn_bv, L0_gnn_wiq, L0_gnn_biq, L0_gnn_wik, L0_gnn_bik, L0_gnn_wiv, L0_gnn_biv, L0_gnn_wo, L0_gnn_bo) + _L0_mix_ref(xn[None], L0_mix_beta, L0_mix_Wq, L0_mix_bq, L0_mix_Wk, L0_mix_bk, L0_mix_Wv, L0_mix_bv, L0_mix_Wo, L0_mix_bo)[0]
    x = x + _L0_ffn_ref(_layernorm(x, axis=-1)[None], L0_ffn_wqkv, L0_ffn_w1, L0_ffn_w2)[0]
    xn = _layernorm(x, axis=-1)
    x = x + _L1_gnn_ref(xn, L1_gnn_W, L1_gnn_a, src, dst) + _L1_mix_ref(xn[None], L1_mix_W_Q, L1_mix_W_K, L1_mix_W_V, L1_mix_W_fc, L1_mix_gamma, L1_mix_beta)[0]
    x = x + _L1_ffn_ref(_layernorm(x, axis=-1)[None], L1_ffn_centroids, L1_ffn_w1, L1_ffn_b1, L1_ffn_w2, L1_ffn_b2, L1_ffn_gamma, L1_ffn_beta)[0]
    return x

_drawn_inputs = setup_inputs


def setup_inputs(seed=0):
    import zlib

    import numpy as np

    out = dict(_drawn_inputs(seed))
    spreads = {'L0_mix_bq': (0.0, 0.8),
     'L0_mix_bk': (0.0, 0.8),
     'L0_mix_bv': (0.0, 0.1),
     'L0_mix_bo': (0.0, 0.1),
     'L1_mix_gamma': (1.0, 0.2),
     'L1_mix_beta': (0.0, 0.1),
     'L1_ffn_b1': (0.0, 0.8),
     'L1_ffn_b2': (0.0, 0.511),
     'L1_ffn_gamma': (1.0, 0.6),
     'L1_ffn_beta': (0.0, 0.8)}
    factors = {'L0_gnn_edge_type_weights': 8.0,
     'L0_gnn_wq': 6.892,
     'L0_gnn_bq': 8.0,
     'L0_gnn_wk': 7.433,
     'L0_gnn_bk': 8.0,
     'L0_gnn_bv': 6.84,
     'L0_gnn_wiq': 7.051,
     'L0_gnn_biq': 8.0,
     'L0_gnn_wik': 7.453,
     'L0_gnn_bik': 8.0,
     'L0_gnn_biv': 4.632,
     'L0_gnn_bo': 3.158,
     'L0_mix_beta': 8.0,
     'L0_mix_Wq': 8.0,
     'L0_mix_Wk': 8.0,
     'L1_gnn_a': 3.96,
     'L1_mix_W_Q': 8.0,
     'L1_mix_W_K': 8.0}
    for name, (base, spread) in spreads.items():
        noise = np.random.default_rng([zlib.crc32(name.encode()), seed]).standard_normal(out[name].shape)
        drawn = base * np.exp(spread * noise) if base else spread * noise
        out[name] = jnp.asarray(drawn.astype(out[name].dtype))
    for name, factor in factors.items():
        out[name] = (out[name] * factor).astype(out[name].dtype)
    return out
```

```python
from contextlib import ExitStack

import numpy as np
import concourse.bass as bass
from concourse import mybir

F32 = mybir.dt.float32
F16 = mybir.dt.float16
BF16 = mybir.dt.bfloat16
I32 = mybir.dt.int32
ALU = mybir.AluOpType
ACT = mybir.ActivationFunctionType
AX = mybir.AxisListType

P = 128
N = 384
NB = N // P
D = 1024
KB = D // P
HEADS = 16
DH = D // HEADS
EDGES = 12288
ET = EDGES // P
GT_ = 8
EG = ET // GT_
F0 = 352
NE = 8
HB0 = NE * F0 // P
F1 = 512
FB1 = F1 // P
SLOTS = 8
EPS = 1e-5
NEG = -1e30

CH_A = 0
CH_B = CH_A + 48
CH_O = CH_B + 24
CH_F0 = CH_O + 16
CH_L1 = CH_F0 + 3 * HB0
CH_F1 = CH_L1 + 40
CHUNKS = CH_F1 + 64

C_BIAS = 0
C_BIV = 64
C_BETA = 72
C_B1 = 80
C_GAM = 112
C_BET = 176
C_EW = 240
NCOLS = 244

T_A = 8
T_B = T_A + 48
T_O = T_B + 16
T_LN2 = T_O + 8
T_GB0 = T_LN2 + 8
T_LN3 = T_GB0 + HB0
T_Q = T_LN3 + 8
T_MIX = T_Q + 8
T_FE = T_MIX + 8
T_XH = T_FE + 8
T_GB1 = T_XH + 8
T_F1 = T_GB1 + NE


class Chain:

    def __init__(self, eng, sem):
        self.eng, self.sem, self.n, self.off = eng, sem, 0, 0

    def __call__(self, ins):
        self.n += 1
        ins.then_inc(self.sem, 1)
        self.eng.wait_ge(self.sem, self.off + self.n)

    def enter(self, turn, per):
        self.mark, self.per, self.off = self.n, per, turn * per

    def leave(self, turns):
        assert self.n - self.mark == self.per, (self.n, self.mark)
        self.n, self.off = self.mark + self.per * turns, 0


def program(nc, x, stream, c32, c16, cols_d, edges_d, sel0_d, sel1_d, wqkv_d, cent_d,
            bo_g, bo_m, a_lr, gam_d, bet_d, b2_d, out):
    with ExitStack() as ctx:
        def sb(name, shape, dt=F32):
            return ctx.enter_context(nc.sbuf_tensor(name, shape, dt))

        def sem(name):
            return ctx.enter_context(nc.semaphore(name))

        ring = sb("ring", [P, SLOTS, 1024])
        xr = sb("xr", [P, NB, D])
        xn = sb("xn", [P, NB, D])
        xnT = sb("xnT", [P, KB, N])
        Y = sb("Y", [P, 6, KB * N])
        G = sb("G", [P, 9216])
        mask = sb("mask", [P, NB, N])
        CT = sb("CT", [P, NB, N])
        rows = sb("rows", [P, 2, D])
        k32 = sb("k32", [P, c32.shape[1]])
        k16 = sb("k16", [P, c16.shape[1]], F16)
        cols = sb("cols", [P, NCOLS])
        scale = sb("scale", [P, 64])
        sbias = sb("sbias", [P, 64])
        ed = sb("ed", [P, 3, ET], I32)
        srcf = sb("srcf", [P, ET])
        dstf = sb("dstf", [P, ET])
        keyf = sb("keyf", [P, ET])
        codef = sb("codef", [P, ET])
        ndup = sb("ndup", [P, ET])
        wts = sb("wts", [P, ET])
        src16 = sb("src16", [P, ET], F16)
        dst16 = sb("dst16", [P, ET], F16)
        zero16 = sb("zero16", [P, 512], BF16)
        wqkv = sb("wqkv", [P, KB, 3 * NE])
        cent = sb("cent", [P, KB, NE])
        GTr = sb("GTr", [NE, N])
        st = sb("st", [P, NB, 12])
        mv = sb("mv", [P, NB, 2])
        ve = sb("ve", [P, NB])
        lnv = sb("lnv", [P, NB])
        rs0 = sb("rs0", [P, NB])
        nwt = sb("nwt", [P, NB])
        rstd = sb("rstd", [P, NB])
        nmx = sb("nmx", [P, 4, NB])
        rsum = sb("rsum", [P, 4, NB])
        rinv = sb("rinv", [P, 4, NB])
        tick = sb("tick", [P, 4 * NB])
        spw = sb("spw", [P, 4, 4])
        al = sb("al", [P, NB])
        ar = sb("ar", [P, NB])
        bank = [ctx.enter_context(nc.psum_tensor(f"bank{i}", [P, 512], F32)) for i in range(8)]

        ident = k32[:, 0:128]
        bdx = k32[:, 128:258]
        bd = k32[:, 128:256]
        later = k32[:, 258:386]
        ones = k32[:, 386:514]
        iota8 = k32[:, 514:538].rearrange("p (b e) -> p b e", b=NB)
        digit = k32[:, 538:538 + ET]
        iota = k16[:, 0:384]
        id16 = k16[:, 384:512]
        id384 = k16[:, 512:640]

        def YT(s):
            return Y[:, s, :].rearrange("p (k n) -> p k n", k=KB)

        def YN(s):
            return Y[:, s, :].rearrange("p (b d) -> p b d", b=NB)

        landed = [sem(f"landed{r}") for r in range(SLOTS)]
        chunk_used = sem("chunk_used")
        x_in = [sem(f"x_in{b}") for b in range(NB)]
        k_in = sem("k_in")
        edge_in = sem("edge_in")
        rows_in = sem("rows_in")
        late_in = sem("late_in")
        sel0_in = sem("sel0_in")
        l1_in = sem("l1_in")
        rows2_in = sem("rows2_in")
        f1_in = sem("f1_in")
        dstep = sem("dstep")
        astep = sem("astep")
        gstep = sem("gstep")
        var_ready = sem("var_ready")
        rstd_seed = sem("rstd_seed")
        xn_ready = sem("xn_ready")
        tp_ready = sem("tp_ready")
        t_evicted = sem("t_evicted")
        beta_exp = sem("beta_exp")
        cols_ready = sem("cols_ready")
        ew_one = sem("ew_one")
        ew_ln = sem("ew_ln")
        bias_added = sem("bias_added")
        edges_ready = sem("edges_ready")
        keys_ready = sem("keys_ready")
        sp_neg = sem("sp_neg")
        sp_exp = sem("sp_exp")
        sp_one = sem("sp_one")
        sp_ln = sem("sp_ln")
        mixprod = sem("mixprod")
        mixs_ready = sem("mixs_ready")
        mixs_taken = sem("mixs_taken")
        oh_ready = sem("oh_ready")
        codes_ready = sem("codes_ready")
        codes_taken = sem("codes_taken")
        group_done = sem("group_done")
        counts_ready = sem("counts_ready")
        ct_done = sem("ct_done")
        m_taken = sem("m_taken")
        mask_ready = sem("mask_ready")
        v2_done = sem("v2_done")
        staged = sem("staged")
        scores_ready = sem("scores_ready")
        scores_read = sem("scores_read")
        exp_done = sem("exp_done")
        pt_ready = sem("pt_ready")
        pt01 = sem("pt01")
        pt2 = sem("pt2")
        av_ready = sem("av_ready")
        av_taken = sem("av_taken")
        x1_done = sem("x1_done")
        mixed_ready = sem("mixed_ready")
        gl_sub = sem("gl_sub")
        gl_exp = sem("gl_exp")
        g2_sub = sem("g2_sub")
        g2_exp = sem("g2_exp")
        gates_ready = sem("gates_ready")
        gt_ready = sem("gt_ready")
        gt_done = sem("gt_done")
        sig_done = sem("sig_done")
        ag_read = sem("ag_read")
        hid_ready = sem("hid_ready")
        acc_ready = sem("acc_ready")
        x2_done = sem("x2_done")
        h_done = sem("h_done")
        diag_ready = sem("diag_ready")
        albc_ready = sem("albc_ready")
        z_ready = sem("z_ready")
        e_ready = sem("e_ready")
        cet_ready = sem("cet_ready")
        k_done = sem("k_done")
        agg_ready = sem("agg_ready")
        agg_taken = sem("agg_taken")
        elu_min = sem("elu_min")
        elu_exp = sem("elu_exp")
        v_done = sem("v_done")
        kv_ready = sem("kv_ready")
        kv_taken = sem("kv_taken")
        num_ready = sem("num_ready")
        num_taken = sem("num_taken")
        zf_done = sem("zf_done")
        aff_ready = sem("aff_ready")
        alpha_done = sem("alpha_done")
        aff_copied = sem("aff_copied")
        xh_ready = sem("xh_ready")
        gate1_ready = sem("gate1_ready")
        gt1_ready = sem("gt1_ready")
        gt1_done = sem("gt1_done")
        he_ready = sem("he_ready")
        relu_done = sem("relu_done")
        hid1_ready = sem("hid1_ready")
        feats_added = sem("feats_added")
        y_ready = sem("y_ready")
        stored = sem("stored")

        junk = CT[:].rearrange("p b n -> p (b n)").bitcast(BF16)[:, 0:GT_ * P].rearrange("p (t n) -> p t n", t=GT_)
        tmp = [G[:, i * 3072:(i + 1) * 3072] for i in range(3)]
        onehot = G[:, :].bitcast(BF16).rearrange("p (q t k n) -> p q t k n", q=2, t=GT_, k=3)
        M = Y[:, 1, 0:2 * NB * N].rearrange("p (h b n) -> p h b n", h=2, b=NB)
        S = G[:, 0:4 * NB * N].rearrange("p (u b n) -> p u b n", u=4, b=NB)
        PT = G[:, 4608:4608 + NB * N].rearrange("p (b n) -> p b n", b=NB)
        qs = G[:, 5760:5760 + 2 * N].rearrange("p (s n) -> p s n", s=2)
        ks = G[:, 6528:6528 + 2 * N].rearrange("p (s n) -> p s n", s=2)
        gate0 = G[:, 0:HB0 * N].rearrange("p (b n) -> p b n", b=HB0)
        sel0 = Y[0:NE, 5, 0:HB0 * P].rearrange("e (b m) -> e b m", b=HB0)
        sg = Y[:, 0, 0:384]
        hpre = Y[:, 0, 384:1152].rearrange("p (b n) -> p b n", b=2)
        hid = Y[:, 0, 1152:1920].rearrange("p (b n) -> p b n", b=2)
        w = Y[:, 1, :]
        kvbd = G[:, 0:8 * 130].rearrange("p (a c) -> p a c", a=8)
        CET = G[:, 1040:1040 + NB * N].rearrange("p (b n) -> p b n", b=NB)
        eT = G[:, 2304:2304 + NB * N].rearrange("p (b n) -> p b n", b=NB)
        dg = G[:, 3456:3456 + NB * P].rearrange("p (b n) -> p b n", b=NB)
        den = G[:, 3840:3840 + 2 * NB].rearrange("p (b j) -> p b j", b=NB)
        rden = G[:, 3850:3850 + 2 * NB].rearrange("p (b j) -> p b j", b=NB)
        rsm = G[:, 3860:3860 + NB]
        rsi = G[:, 3864:3864 + NB]
        a_l = Y[:, 5, 0:1024]
        a_r = Y[:, 5, 1024:2048]
        prod = Y[:, 5, 2048:3072]
        sel1 = G[0:NE, 0:NE * P].rearrange("e (b m) -> e b m", b=NE)
        b2 = G[0:NE, 1024:2048]
        gate1 = YT(4)
        rl = G[:, 2048:2048 + 2 * N].rearrange("p (s n) -> p s n", s=2)
        hid1 = G[:, 3072:3072 + FB1 * N].rearrange("p (b n) -> p b n", b=FB1)

        block = ctx.enter_context(nc.Block())

        @block.sync
        def _(sp):
            for b in range(NB):
                sp.dma_start(xr[:, b, :], x[b * P:(b + 1) * P, :]).then_inc(x_in[b], 16)

            def load(r, c):
                sp.dma_start(ring[:, r, :], stream[c]).then_inc(landed[r], 16)

            for r in range(SLOTS):
                load(r, r)
            with sp.Fori(1, CH_F0 // 8) as g:
                for r in range(SLOTS):
                    sp.wait_ge(chunk_used, 8 * g - 7 + r)
                    load(r, 8 * g + r)
            for j in range(4):
                sp.wait_ge(chunk_used, CH_F0 - 8 + j + 1)
                load(j, CH_F0 + j)
            c = CH_F0 + 4
            for j in range(6):
                sp.wait_ge(chunk_used, CH_F0 + j + 1 if j < 4 else CH_F0 - 8 + j + 1)
                load(j, c + j)
            with sp.Fori(2, HB0 // 2) as i:
                for j in range(6):
                    sp.wait_ge(chunk_used, c - 11 + 6 * i + j)
                    load(j, c - 6 + 6 * i + j)
            e = c + 6 * (HB0 // 2 - 1)
            for j in range(2):
                sp.wait_ge(chunk_used, e - 6 + j + 1)
                load(j, e + j)
            for r in range(SLOTS):
                sp.wait_ge(chunk_used, e + r + 1 if r < 2 else (e - 6 + r + 1 if r < 6 else CH_F0 - 8 + r + 1))
                load(r, CH_L1 + r)
            with sp.Fori(1, (CHUNKS - CH_L1) // 8) as g:
                for r in range(SLOTS):
                    sp.wait_ge(chunk_used, CH_L1 - 7 + 8 * g + r)
                    load(r, CH_L1 + 8 * g + r)
            for n in range(6):
                half, b = n // NB, n % NB
                sp.wait_ge(y_ready, n + 1)
                sp.dma_start(out[b * P:(b + 1) * P, half * 512:(half + 1) * 512],
                             xr[:, b, half * 512:(half + 1) * 512]).then_inc(stored, 16)
            sp.wait_ge(stored, 96)

        @block.gpsimd
        def _(pool):
            step = Chain(pool, gstep)
            pool.wait_ge(rows_in, 32)
            step(pool.tensor_tensor(rows[:, 0, :], rows[:, 0, :], rows[:, 1, :], ALU.add))
            pool.wait_ge(xn_ready, NB)
            for b in range(NB):
                pool.tensor_tensor(xr[:, b, :], xr[:, b, :], rows[:, 0, :], ALU.add).then_inc(bias_added, 1)
            pool.wait_ge(bias_added, NB)
            pool.dma_start(rows[:, 0, :], gam_d.to_broadcast([P, D])).then_inc(rows2_in, 16)
            pool.dma_start(rows[:, 1, :], bet_d.to_broadcast([P, D])).then_inc(rows2_in, 16)
            for p in range(2):
                pool.wait_ge(t_evicted, T_B + 8 + p + 1)
                if p == 0:
                    pool.wait_ge(mask_ready, 1)
                pool.tensor_copy(qs[:, p, :], YT(0)[:, p, :])
                pool.tensor_copy(ks[:, p, :], YT(1)[:, p, :]).then_inc(staged, 1)
            pool.wait_ge(t_evicted, T_O)
            with pool.Fori(1, 4) as i:
                for p in range(2):
                    pool.wait_ge(scores_ready, 12 * i - 12 + 6 * p + 6)
                    pool.tensor_copy(qs[:, p, :], Y[:, 0, bass.ds((2 * i + p) * N, N)])
                    pool.tensor_copy(ks[:, p, :], Y[:, 1, bass.ds((2 * i + p) * N, N)]).then_inc(staged, 1)
            pool.wait_ge(chunk_used, CH_B + 24)
            pool.dma_start(sel0, sel0_d).then_inc(sel0_in, 16)
            pool.wait_ge(t_evicted, T_LN3)
            pool.dma_start(Y[:, 5, 0:2048], a_lr.to_broadcast([P, 2 * D])).then_inc(l1_in, 16)
            pool.wait_ge(zf_done, 6)
            pool.wait_ge(t_evicted, T_FE)
            pool.dma_start(sel1, sel1_d).then_inc(f1_in, 16)
            pool.dma_start(b2, b2_d).then_inc(f1_in, 16)
            pool.wait_ge(xh_ready, NB)
            for b in range(NB):
                pool.tensor_tensor(xr[:, b, :], xr[:, b, :], xn[:, b, :], ALU.add).then_inc(feats_added, 1)

        @block.scalar
        def _(act):
            step = Chain(act, astep)
            act.dma_start(ed[:], edges_d).then_inc(edge_in, 16)
            act.dma_start(k32[:], c32).then_inc(k_in, 16)
            act.dma_start(k16[:], c16).then_inc(k_in, 16)
            act.dma_start(cols[:], cols_d).then_inc(k_in, 16)
            act.dma_start(rows[:, 0, :], bo_g.to_broadcast([P, D])).then_inc(rows_in, 16)
            act.dma_start(rows[:, 1, :], bo_m.to_broadcast([P, D])).then_inc(rows_in, 16)
            act.dma_start(wqkv[:], wqkv_d).then_inc(late_in, 16)
            act.dma_start(cent[:], cent_d).then_inc(late_in, 16)

            def seed(c):
                act.wait_ge(var_ready, c + 1)
                step(act.activation(lnv[:], ve[:], ACT.Ln))
                act.activation(rs0[:], lnv[:], ACT.Exp, scale=-0.5).then_inc(rstd_seed, 1)

            def evict_transposes(base, first, dst, bias=None):
                for m in range(KB):
                    act.wait_ge(tp_ready, first + m + 1)
                    b = bank[(base + m) % 2][:, 0:N]
                    if bias is None:
                        act.activation(dst[:, m, :], b, ACT.Copy).then_inc(t_evicted, 1)
                    else:
                        act.activation(dst[:, m, :], b, ACT.Identity,
                                       bias=cols[:, bias + m:bias + m + 1]).then_inc(t_evicted, 1)

            act.wait_ge(k_in, 48)
            act.activation(scale[:, 0:8], cols[:, C_BETA:C_BETA + 8], ACT.Exp, scale=-1.0).then_inc(beta_exp, 1)
            act.activation(spw[:, 1, :], cols[:, C_EW:C_EW + 4], ACT.Abs)
            step(act.activation(spw[:, 0, :], cols[:, C_EW:C_EW + 4], ACT.Copy))
            act.activation(spw[:, 2, :], spw[:, 1, :], ACT.Exp, scale=-1.0).then_inc(beta_exp, 1)
            seed(0)
            act.wait_ge(ew_one, 1)
            act.activation(spw[:, 1, :], spw[:, 3, :], ACT.Ln).then_inc(ew_ln, 1)
            evict_transposes(0, 0, xnT)

            def evict_T(layer, m, zero_based=True):
                if isinstance(layer, int):
                    dst = Y[:, layer, m * N:(m + 1) * N]
                    sc = scale[:, layer * 8 + m:layer * 8 + m + 1]
                    bi = sbias[:, layer * 8 + m:layer * 8 + m + 1]
                else:
                    dst = Y[:, bass.ds(layer, 1), m * N:(m + 1) * N].rearrange("p a n -> p (a n)")
                    sc = scale[:, bass.ds(layer * 8 + m, 1)]
                    bi = sbias[:, bass.ds(layer * 8 + m, 1)]
                act.wait_ge(chunk_used, layer * 8 + m + 1)
                act.activation(dst, bank[m % 2][:, 0:N], ACT.Identity, bias=bi, scale=sc).then_inc(t_evicted, 1)

            act.wait_ge(cols_ready, 1)
            for m in range(KB):
                evict_T(0, m)
            with act.Fori(0, 2) as s:
                for m in range(3):
                    evict_T(s + 1, m)
                act.wait_ge(sp_neg, s + 1)
                act.activation(tmp[1], tmp[0], ACT.Exp).then_inc(sp_exp, 1)
                for m in range(3, 6):
                    evict_T(s + 1, m)
                act.wait_ge(sp_one, s + 1)
                act.activation(tmp[2], tmp[0], ACT.Ln).then_inc(sp_ln, 1)
                for m in range(6, 8):
                    evict_T(s + 1, m)
            with act.Fori(3, 6) as layer:
                for m in range(KB):
                    evict_T(layer, m)

            act.wait_ge(counts_ready, 1)
            for b in range(NB):
                act.activation(CT[:, b, :], bank[5 + b][:, 0:N], ACT.Copy).then_inc(ct_done, 1)

            act.wait_ge(mixs_taken, 8)
            act.wait_ge(m_taken, 1)
            with act.Fori(0, 2) as j:
                for m in range(KB):
                    act.wait_ge(chunk_used, CH_B + 8 * j + m + 1)
                    act.activation(Y[:, bass.ds(j, 1), m * N:(m + 1) * N].rearrange("p a n -> p (a n)"),
                                   bank[m % 2][:, 0:N], ACT.Identity,
                                   bias=sbias[:, bass.ds(j * 8 + 48 + m, 1)],
                                   scale=scale[:, bass.ds(j * 8 + 48 + m, 1)]).then_inc(t_evicted, 1)

            def evict_N(base, dst, func, done):
                for half in range(2):
                    act.wait_ge(chunk_used, base + 4 * half + 4)
                    for b in range(NB):
                        act.activation(dst[:, b, half * 512:(half + 1) * 512],
                                       bank[2 + 3 * half + b][:], func).then_inc(done, 1)

            evict_N(CH_B + 16, YN(3), ACT.Copy, v2_done)

            def exps(h, u):
                for b in range(NB):
                    act.wait_ge(scores_read, 3 * h + b + 1)
                    act.activation(S[:, u, b, :], S[:, u, b, :], ACT.Exp, scale=-1.0, bias=nmx[:, u, b:b + 1],
                                   accum_out=rsum[:, u, b:b + 1]).then_inc(exp_done, 1)

            def turn_out(h, first=False):
                for mb in range(2):
                    act.wait_ge(pt_ready, 3 * h + mb + 1)
                    if mb == 0 and not first:
                        act.wait_ge(av_ready, h)
                    act.activation(PT[:, mb, :], bank[5 + mb][:, 0:N], ACT.Copy).then_inc(pt01, 1)

            exps(0, 0)
            exps(1, 1)
            for u in range(4):
                turn_out(u, u == 0)
                exps(u + 2, (u + 2) % 4)
            with act.Fori(1, 3) as i:
                for u in range(4):
                    turn_out(4 * i + u)
                    exps(4 * i + u + 2, (u + 2) % 4)
            for u in range(4):
                turn_out(12 + u)
                if u < 2:
                    exps(14 + u, u + 2)

            evict_transposes(T_O, 8, YT(4), bias=C_BIV)
            seed(1)
            evict_transposes(T_LN2, 16, xnT)

            act.wait_ge(gl_sub, 1)
            act.activation(w[:, 200:392], w[:, 200:392], ACT.Exp).then_inc(gl_exp, 1)
            act.wait_ge(g2_sub, 1)
            act.activation(w[:, 0:3], w[:, 0:3], ACT.Exp).then_inc(g2_exp, 1)
            for n in range(HB0):
                act.wait_ge(tp_ready, 24 + n + 1)
                act.activation(gate0[:, n, :], bank[(T_GB0 + n) % 2][:, 0:N], ACT.Copy).then_inc(t_evicted, 1)
            def sig(used, n, first=False):
                act.wait_ge(chunk_used, used)
                if not first:
                    act.wait_ge(ag_read, n)
                act.activation(sg, bank[0][:, 0:N], ACT.Sigmoid).then_inc(sig_done, 1)

            sig(CH_F0 + 1, 0, True)
            sig(CH_F0 + 3, 1)
            with act.Fori(1, HB0 // 2) as i:
                sig(CH_F0 - 2 + 6 * i + 1, 2 * i)
                sig(CH_F0 - 2 + 6 * i + 4, 2 * i + 1)

            seed(2)
            evict_transposes(T_LN3, 24 + HB0, xnT)
            evict_N(CH_L1, YN(0), ACT.Copy, h_done)
            for m in range(KB):
                act.wait_ge(chunk_used, CH_L1 + 8 + m + 1)
                act.activation(YT(1)[:, m, :], bank[m % 2][:, 0:N], ACT.Sigmoid).then_inc(t_evicted, 1)
            act.wait_ge(z_ready, 1)
            act.activation(eT[:], eT[:], ACT.Exp).then_inc(e_ready, 1)
            evict_N(CH_L1 + 16, YN(2), ACT.Sigmoid, k_done)
            act.wait_ge(elu_min, 1)
            act.activation(Y[:, 5, :], Y[:, 5, :], ACT.Exp).then_inc(elu_exp, 1)
            evict_N(CH_L1 + 24, YN(3), ACT.Copy, v_done)
            act.wait_ge(kv_taken, 8)
            evict_transposes(T_MIX, 32 + HB0, YT(1))
            seed(3)
            seed(4)
            evict_transposes(T_FE, 40 + HB0, xnT)
            seed(5)
            act.wait_ge(aff_copied, 1)
            act.activation(w[:, 24:48], w[:, 0:24], ACT.Sigmoid).then_inc(alpha_done, 1)
            evict_transposes(T_XH, 48 + HB0, YT(2))
            for n in range(NE):
                act.wait_ge(tp_ready, 56 + HB0 + n + 1)
                act.activation(gate1[:, n, :], bank[(T_GB1 + n) % 2][:, 0:N], ACT.Copy).then_inc(t_evicted, 1)
            def relu(e, f):
                act.wait_ge(chunk_used, 8 * e + f + CH_F1 + 1)
                act.activation(rl[:, f % 2, :], bank[f % 2][:, 0:N], ACT.Relu,
                               bias=cols[:, bass.ds(4 * e + C_B1 + f, 1)]).then_inc(t_evicted, 1)
            for f in range(FB1):
                if f >= 2:
                    act.wait_ge(hid1_ready, f - 1)
                relu(0, f)
            with act.Fori(1, NE) as e:
                for f in range(FB1):
                    act.wait_ge(hid1_ready, 4 * e + f - 1)
                    relu(e, f)

        @block.tensor
        def _(pe):
            def transposes(base, src, dst_blocks=KB):
                for m in range(KB):
                    n = base + m
                    if n >= 2:
                        pe.wait_ge(t_evicted, n - 1)
                    for b in range(NB):
                        last = pe.transpose(bank[n % 2][:, b * P:(b + 1) * P], src[:, b, m * P:(m + 1) * P], ident)
                    last.then_inc(tp_ready, 1)

            def chunk_T(r, rhs, free, arrived, to):
                pe.wait_ge(landed[r], arrived)
                pe.wait_ge(t_evicted, free)
                for k in range(KB):
                    last = pe.matmul(bank[to][:, 0:N], ring[:, r, k * P:(k + 1) * P], rhs(k),
                                     start=(k == 0), stop=(k == KB - 1))
                last.then_inc(chunk_used, 1)

            def chunk_N(r, lhs, k0, half, arrived, start, stop):
                pe.wait_ge(landed[r], arrived)
                for k in range(2):
                    for b in range(NB):
                        last = pe.matmul(bank[2 + 3 * half + b][:], lhs(k0 + k, b),
                                         ring[:, r, k * 512:(k + 1) * 512],
                                         start=(start and k == 0), stop=(stop and k == 1), skip_group_check=True)
                last.then_inc(chunk_used, 1)

            def layer_N(g, lhs, arrived, wait_half):
                for half in range(2):
                    wait_half(half)
                    for kk in range(4):
                        r = 4 * half + kk
                        chunk_N(r, lhs, 2 * kk, half, arrived(r), kk == 0, kk == 3)

            def tok(area):
                v = YT(area)
                return lambda k, b: v[:, k, b * P:(b + 1) * P]

            def xtok(k, b):
                return xnT[:, k, b * P:(b + 1) * P]

            pe.wait_ge(k_in, 48)
            pe.wait_ge(xn_ready, NB)
            transposes(0, xn)
            pe.wait_ge(t_evicted, T_A)

            def keys(layer):
                pe.wait_ge(edges_ready, 2 * layer + 2)
                for g in range(2):
                    for t in range(GT_):
                        dst = bank[4 + 2 * g + t // 4][:, (t % 4) * P:(t % 4 + 1) * P]
                        e = layer * 16 + g * 8 + t
                        pe.matmul(dst, src16[:, bass.ds(e, 1)].to_broadcast([P, P]), id384, start=True, stop=False)
                        last = pe.matmul(dst, dst16[:, bass.ds(e, 1)].to_broadcast([P, P]), id16,
                                         start=False, stop=True)
                    last.then_inc(keys_ready, 1)

            def layer_A(layer, before=None):
                keys(layer)
                for m in range(KB):
                    if before:
                        before(m)
                    chunk_T(m, lambda k: xnT[:, k, :], layer * 8 + m + T_A - 1, layer * 16 + 16, m % 2)

            with pe.Fori(0, 5) as layer:
                layer_A(layer)

            def head_sums(m):
                if m == 0:
                    pe.wait_ge(mixprod, 1)
                if m >= 2:
                    pe.wait_ge(mixs_taken, m - 1)
                pe.matmul(bank[2 + m % 2][:, 0:N], bd, YT(0)[:, m, :], start=True, stop=True).then_inc(mixs_ready, 1)

            layer_A(5, head_sums)

            pe.wait_ge(mixs_taken, 8)
            pe.wait_ge(edges_ready, 2 + EG)
            for b in range(NB):
                pe.matmul(bank[5 + b][:, 0:N], zero16[:, 0:P], zero16[:, 0:N], start=True, stop=False,
                          skip_group_check=True)
            with pe.Fori(0, EG // 2) as i:
                for q in range(2):
                    g = 2 * i + q
                    pe.wait_ge(codes_taken, 3 * g + 3)
                    for t in range(GT_):
                        pe.wait_ge(oh_ready, 8 * g + t + 1)
                        for b in range(NB):
                            last = pe.matmul(bank[2 + b][:, 0:N], onehot[:, q, t, 1, b * P:(b + 1) * P],
                                             onehot[:, q, t, 2, :], start=(t == 0), stop=(t == GT_ - 1),
                                             skip_group_check=True)
                    last.then_inc(codes_ready, 1)
                    for t in range(GT_):
                        for b in range(NB):
                            last = pe.matmul(bank[5 + b][:, 0:N], onehot[:, q, t, 2, b * P:(b + 1) * P],
                                             onehot[:, q, t, 0, :], start=False, stop=False, skip_group_check=True)
                    last.then_inc(group_done, 1)
            for b in range(NB):
                last = pe.matmul(bank[5 + b][:, 0:N], zero16[:, 0:P], zero16[:, 0:N], start=False, stop=True,
                                 skip_group_check=True)
            last.then_inc(counts_ready, 1)

            with pe.Fori(0, 2) as j:
                for m in range(KB):
                    chunk_T(m, lambda k: Y[:, bass.ds(j + 3, 1), k * N:(k + 1) * N].rearrange("p a n -> p (a n)"),
                            8 * j + m + T_B - 1, 16 * j + 16 * (CH_B // 8 + 1), m % 2)

            def free_b(half):
                if half == 0:
                    pe.wait_ge(codes_taken, 3 * EG + 3)
                else:
                    pe.wait_ge(ct_done, NB)
            layer_N(0, tok(5), lambda r: 16 * (CH_B // 8 + 3), free_b)

            def scores(h, u, first=False):
                o = 64 * (u % 2)
                for b in range(NB):
                    if not first:
                        pe.wait_ge(scores_read, 3 * h - 3 + b + 1)
                    last = pe.matmul(bank[2 + b][:, 0:N], qs[o:o + 64, u // 2, b * P:(b + 1) * P],
                                     ks[o:o + 64, u // 2, :], start=True, stop=True).then_inc(scores_ready, 1)

            def turn(h, u, first=False):
                pe.wait_ge(exp_done, 3 * h + 3)
                for mb in range(NB):
                    if not first:
                        if mb < 2:
                            pe.wait_ge(pt01, 2 * h - 2 + mb + 1)
                        else:
                            pe.wait_ge(pt2, h)
                    for b in range(NB):
                        last = pe.transpose(bank[5 + mb][:, b * P:(b + 1) * P], S[:, u, b, mb * P:(mb + 1) * P], ident)
                    last.then_inc(pt_ready, 1)

            def weigh(h, u, first=False):
                pe.wait_ge(pt01, 2 * h + 2)
                pe.wait_ge(pt2, h + 1)
                if not first:
                    pe.wait_ge(av_taken, h - 1)
                for b in range(NB):
                    for mb in range(NB):
                        last = pe.matmul(bank[u % 2][:, b * DH:(b + 1) * DH], PT[:, mb, b * P:(b + 1) * P],
                                         Y[:, 3, bass.ds(h * DH + mb * D, DH)], start=(mb == 0), stop=(mb == NB - 1))
                last.then_inc(av_ready, 1)

            pe.wait_ge(v2_done, 6)
            pe.wait_ge(t_evicted, T_O)
            pe.wait_ge(staged, 1)
            scores(0, 0, True)
            scores(1, 1)
            for u in range(4):
                turn(u, u, u == 0)
                if u == 0 or u == 2:
                    pe.wait_ge(staged, u // 2 + 2)
                scores(u + 2, (u + 2) % 4)
                weigh(u, u, u < 2)
            with pe.Fori(1, 3) as i:
                for u in range(4):
                    turn(4 * i + u, u)
                    if u == 0 or u == 2:
                        pe.wait_ge(staged, 2 * i + u // 2 + 2)
                    scores(4 * i + u + 2, (u + 2) % 4)
                    weigh(4 * i + u, u)
            for u in range(4):
                turn(12 + u, u)
                if u == 0:
                    pe.wait_ge(staged, 8)
                if u < 2:
                    scores(14 + u, u + 2)
                weigh(12 + u, u)

            pe.wait_ge(scores_read, 48)
            for kk in range(4):
                chunk_N(kk, tok(2), 2 * kk, 0, 16 * (CH_O // 8 + 1), kk == 0, False)
            pe.wait_ge(av_taken, HEADS)
            transposes(T_O, xn)
            pe.wait_ge(t_evicted, T_O + 8)
            for kk in range(4):
                chunk_N(4 + kk, tok(4), 2 * kk, 0, 16 * (CH_O // 8 + 1), False, kk == 3)
            pe.wait_ge(pt01, 32)
            pe.wait_ge(pt2, 16)
            for kk in range(4):
                chunk_N(kk, tok(2), 2 * kk, 1, 16 * (CH_O // 8 + 2), kk == 0, False)
            for kk in range(4):
                chunk_N(4 + kk, tok(4), 2 * kk, 1, 16 * (CH_O // 8 + 2), False, kk == 3)

            pe.wait_ge(xn_ready, 2 * NB)
            transposes(T_LN2, xn)
            pe.wait_ge(late_in, 32)
            pe.wait_ge(t_evicted, T_LN2 + 8)
            for b in range(NB):
                for k in range(KB):
                    last = pe.matmul(bank[2][:, b * 24:(b + 1) * 24], xtok(k, b), wqkv[:, k, :],
                                     start=(k == 0), stop=(k == KB - 1))
            last.then_inc(mixed_ready, 1)
            pe.wait_ge(gates_ready, 1)
            for b in range(NB):
                last = pe.transpose(bank[3][0:NE, b * P:(b + 1) * P], w[:, 72 + b * 8:72 + (b + 1) * 8], ident)
            last.then_inc(gt_ready, 1)
            pe.wait_ge(gt_done, 1)
            pe.wait_ge(sel0_in, 16)
            for n in range(HB0):
                if n >= 2:
                    pe.wait_ge(t_evicted, T_GB0 + n - 1)
                pe.matmul(bank[(T_GB0 + n) % 2][:, 0:N], sel0[:, n, :], GTr[:], start=True, stop=True)\
                    .then_inc(tp_ready, 1)
            for n in range(6):
                pe.matmul(bank[2 + n][:], zero16[:, 0:P], zero16[:], start=True, stop=False, skip_group_check=True)

            def up0(r, arrived, n, first=False):
                if not first:
                    pe.wait_ge(ag_read, n)
                for s in range(2):
                    pe.wait_ge(landed[r + s], arrived(r + s))
                    for k in range(KB):
                        last = pe.matmul(bank[s][:, 0:N], ring[:, r + s, k * P:(k + 1) * P], xnT[:, k, :],
                                         start=(k == 0), stop=(k == KB - 1))
                    last.then_inc(chunk_used, 1)

            def down0(r, half, arrived, n):
                pe.wait_ge(hid_ready, n)
                chunk_N(r, lambda k, b: hid[:, k, b * P:(b + 1) * P], 0, half, arrived, False, False)

            pe.wait_ge(t_evicted, T_LN3)
            u0 = CH_F0 // 8
            up0(0, lambda r: 16 * (u0 + 1), 0, True)
            up0(2, lambda r: 16 * (u0 + 1), 1)
            with pe.Fori(1, HB0 // 2) as i:
                def arr0(r):
                    return 16 * i + 16 * (u0 + 1 if r < 4 else u0)
                up0(0, arr0, 2 * i)
                down0(2, 0, arr0(2), 2 * i)
                up0(3, arr0, 2 * i + 1)
                down0(5, 1, arr0(5), 2 * i)
            down0(0, 0, 16 * (u0 + 12), HB0)
            down0(1, 1, 16 * (u0 + 12), HB0)
            for n in range(6):
                pe.matmul(bank[2 + n][:], zero16[:, 0:P], zero16[:], start=False, stop=True,
                          skip_group_check=True).then_inc(acc_ready, 1)

            uses = [u0 + 12, u0 + 12, u0 + 11, u0 + 11, u0 + 10, u0 + 10, u0, u0]

            def arr(g):
                return lambda r: 16 * (uses[r] + g + 1)

            pe.wait_ge(xn_ready, 3 * NB)
            transposes(T_LN3, xn)
            pe.wait_ge(t_evicted, T_LN3 + 8)
            layer_N(0, xtok, arr(0), lambda half: pe.wait_ge(x2_done, 6))
            for m in range(KB):
                chunk_T(m, lambda k: xnT[:, k, :], T_Q + m - 1, arr(1)(m), m % 2)
            pe.wait_ge(diag_ready, 1)
            pe.wait_ge(t_evicted, T_MIX)
            for b in range(NB):
                last = pe.matmul(bank[0][:, b * P:(b + 1) * P], ones, dg[:, b, :], start=True, stop=True)
            last.then_inc(albc_ready, 1)
            layer_N(0, xtok, arr(2), lambda half: pe.wait_ge(h_done, 6))
            pe.wait_ge(cet_ready, 1)
            pe.wait_ge(k_done, 6)
            for b in range(NB):
                for db in range(NB):
                    pe.matmul(bank[1][:, b:b + 1], CET[:, db, b * P:(b + 1) * P], ones[:, 0:1],
                              start=(db == 0), stop=(db == NB - 1))
            h = YN(0)
            for b in range(NB):
                for half in range(2):
                    for db in range(NB):
                        last = pe.matmul(bank[2 + 3 * half + b][:], CET[:, db, b * P:(b + 1) * P],
                                         h[:, db, half * 512:(half + 1) * 512], start=(db == 0), stop=(db == NB - 1))
                last.then_inc(agg_ready, 1)
            layer_N(0, xtok, arr(3), lambda half: pe.wait_ge(agg_taken, NB))
            K, V = YN(2), YN(3)
            pe.wait_ge(v_done, 6)
            for a in range(8):
                if a >= 2:
                    pe.wait_ge(kv_taken, a - 1)
                for b in range(NB):
                    pe.matmul(bank[a % 2][:, 0:P], K[:, b, a * P:(a + 1) * P], V[:, b, a * P:(a + 1) * P],
                              start=(b == 0), stop=(b == NB - 1))
                for b in range(NB):
                    last = pe.matmul(bank[a % 2][:, P:P + 2], K[:, b, a * P:(a + 1) * P], ones[:, 0:2],
                                     start=(b == 0), stop=(b == NB - 1))
                last.then_inc(kv_ready, 1)
            for a in range(8):
                pe.wait_ge(kv_taken, 8)
                if a >= 2:
                    pe.wait_ge(num_taken, a - 1)
                for b in range(NB):
                    last = pe.matmul(bank[a % 2][:, b * 130:(b + 1) * 130], YT(1)[:, a, b * P:(b + 1) * P],
                                     kvbd[:, a, :], start=True, stop=True)
                last.then_inc(num_ready, 1)
            pe.wait_ge(num_taken, 8)
            transposes(T_MIX, YN(2))
            pe.wait_ge(t_evicted, T_MIX + 8)
            layer_N(0, tok(1), arr(4), lambda half: None)

            pe.wait_ge(xn_ready, 4 * NB)
            transposes(T_FE, xn)
            pe.wait_ge(t_evicted, T_FE + 8)
            pe.wait_ge(zf_done, 6)
            for b in range(NB):
                for k in range(KB):
                    last = pe.matmul(bank[2][:, b * 8:(b + 1) * 8], xtok(k, b), cent[:, k, :],
                                     start=(k == 0), stop=(k == KB - 1))
            last.then_inc(aff_ready, 1)
            pe.wait_ge(xh_ready, NB)
            transposes(T_XH, YN(0))
            pe.wait_ge(gate1_ready, 1)
            for b in range(NB):
                last = pe.transpose(bank[3][0:NE, b * P:(b + 1) * P], w[:, 72 + b * 8:72 + (b + 1) * 8], ident)
            last.then_inc(gt1_ready, 1)
            pe.wait_ge(gt1_done, 1)
            pe.wait_ge(f1_in, 32)
            for n in range(NE):
                pe.wait_ge(t_evicted, T_GB1 + n - 1)
                pe.matmul(bank[(T_GB1 + n) % 2][:, 0:N], sel1[:, n, :], GTr[:], start=True, stop=True)\
                    .then_inc(tp_ready, 1)
            for half in range(2):
                for b in range(NB):
                    pe.matmul(bank[2 + 3 * half + b][:], GTr[:, b * P:(b + 1) * P], b2[:, half * 512:(half + 1) * 512],
                              start=True, stop=False, skip_group_check=True)
            with pe.Fori(0, NE) as e:
                pe.wait_ge(he_ready, e + 1)
                for f in range(FB1):
                    chunk_T(f, lambda k: YT(3)[:, k, :], 4 * e + T_F1 + f - 1, 16 * e + arr(5)(f), f % 2)
                for kk in range(2):
                    pe.wait_ge(hid1_ready, 4 * e + 2 * kk + 2)
                    for half in range(2):
                        r = 4 + 2 * kk + half
                        chunk_N(r, lambda k, b: hid1[:, k, b * P:(b + 1) * P], 2 * kk, half,
                                16 * e + arr(5)(r), False, False)
            for n in range(6):
                pe.matmul(bank[2 + n][:], zero16[:, 0:P], zero16[:], start=False, stop=True,
                          skip_group_check=True).then_inc(acc_ready, 1)

        @block.vector
        def _(v):
            step = Chain(v, dstep)
            tt, ts, stt = v.tensor_tensor, v.tensor_scalar, v.scalar_tensor_tensor

            def rstds(c, src, waits=None):
                for b in range(NB):
                    if waits:
                        waits(b)
                    v.bn_stats(st[:, b, 0:6], src[:, b, 0:512])
                    step(v.bn_stats(st[:, b, 6:12], src[:, b, 512:1024]))
                    last = v.bn_aggr(mv[:, b, :], st[:, b, :])
                step(last)
                ts(ve[:], mv[:, :, 1], EPS, None, ALU.add).then_inc(var_ready, 1)
                v.wait_ge(var_ready, c + 1)
                v.wait_ge(rstd_seed, c + 1)
                step(tt(nwt[:], rs0[:], rs0[:], ALU.mult))
                step(tt(nwt[:], nwt[:], ve[:], ALU.mult))
                step(ts(nwt[:], nwt[:], -0.5, 1.5, ALU.mult, ALU.add))
                step(tt(rstd[:], rs0[:], nwt[:], ALU.mult))

            def normalise(dst, src, done):
                for b in range(NB):
                    ts(dst[:, b, :], src[:, b, :], mv[:, b, 0:1], rstd[:, b:b + 1],
                       ALU.subtract, ALU.mult).then_inc(done, 1)

            v.memset(zero16[:], 0.0)
            v.wait_ge(edge_in, 16)
            v.tensor_copy(srcf[:], ed[:, 0, :])
            v.tensor_copy(dstf[:], ed[:, 1, :])
            v.tensor_copy(src16[:], ed[:, 0, :])
            v.tensor_copy(dst16[:], ed[:, 1, :])
            step(v.tensor_copy(codef[:], ed[:, 2, :]))
            v.wait_ge(k_in, 48)
            step(stt(keyf[:], srcf[:], float(N), dstf[:], ALU.mult, ALU.add))
            step(ts(wts[:], codef[:], 0.0, 4.0, ALU.is_equal, ALU.mult))
            step(tt(codef[:], codef[:], wts[:], ALU.add))
            stt(codef[:], codef[:], 3.0, digit, ALU.add, ALU.mult).then_inc(edges_ready, 2)
            v.wait_ge(edges_ready, 2)

            for b in range(NB):
                v.wait_ge(x_in[b], 16)
            rstds(0, xr)
            normalise(xn, xr, xn_ready)

            v.wait_ge(beta_exp, 2)
            ts(spw[:, 3, :], spw[:, 2, :], 1.0, None, ALU.add).then_inc(ew_one, 1)
            step(ts(scale[:, 0:8], scale[:, 0:8], 0.125, None, ALU.mult))
            step(v.tensor_copy(scale[:, 8:16], scale[:, 0:8]))
            v.memset(scale[:, 16:48], 1.0)
            v.memset(scale[:, 48:56], DH ** -0.5)
            step(v.memset(scale[:, 56:64], 1.0))
            tt(sbias[:], cols[:, C_BIAS:C_BIAS + 64], scale[:], ALU.mult).then_inc(cols_ready, 1)
            v.wait_ge(ew_one, 1)
            v.wait_ge(ew_ln, 1)
            step(stt(spw[:, 3, :], spw[:, 3, :], -1.0, spw[:, 2, :], ALU.add, ALU.subtract))
            step(tt(spw[:, 1, :], spw[:, 1, :], spw[:, 3, :], ALU.subtract))
            step(stt(spw[:, 0, :], spw[:, 0, :], 0.0, spw[:, 1, :], ALU.max, ALU.add))

            def dedup(group, q):
                v.wait_ge(keys_ready, group + 1)
                v.wait_ge(edges_ready, group + 2)
                for t in range(GT_):
                    e = group * 8 + t
                    src = bank[4 + 2 * q + t // 4][:, (t % 4) * P:(t % 4 + 1) * P]
                    last = stt(junk[:, t, :], src, keyf[:, bass.ds(e, 1)], later, ALU.is_equal, ALU.mult,
                               accum_out=ndup[:, bass.ds(e, 1)])
                last.then_inc(edges_ready, 1)

            def dedups(layer):
                for q in range(2):
                    dedup(layer * 2 + q, q)

            dedups(0)
            with v.Fori(0, 2) as s:
                step.enter(s, 3)
                v.wait_ge(t_evicted, 8 * s + T_A + 8)
                z = Y[:, bass.ds(s, 1), :].rearrange("p a n -> p (a n)")
                stt(tmp[0], z, -1.0, z, ALU.mult, ALU.min).then_inc(sp_neg, 1)
                dedups(s + 1)
                v.wait_ge(sp_exp, s + 1)
                ts(tmp[0], tmp[1], 1.0, None, ALU.add).then_inc(sp_one, 1)
                v.wait_ge(sp_one, s + 1)
                v.wait_ge(sp_ln, s + 1)
                step(stt(tmp[0], tmp[0], -1.0, tmp[1], ALU.add, ALU.subtract))
                step(tt(tmp[2], tmp[2], tmp[0], ALU.subtract))
                step(stt(z, z, 0.0, tmp[2], ALU.max, ALU.add))
                step.leave(2)
            tt(Y[:, 0, :], Y[:, 0, :], Y[:, 1, :], ALU.mult).then_inc(mixprod, 1)
            with v.Fori(3, 6) as layer:
                dedups(layer)
            v.wait_ge(edges_ready, 2 + EG)
            step(stt(wts[:], ndup[:], 0.0, codef[:], ALU.is_equal, ALU.mult))
            v.wait_ge(mixprod, 1)
            v.memset(M[:], 0.0).then_inc(codes_taken, 3)

            for m in range(KB):
                v.wait_ge(mixs_ready, m + 1)
                s_ = bank[2 + m % 2][:, 0:N]
                r_ = tmp[0][:, m * N:(m + 1) * N]
                step(v.reciprocal(r_, s_))
                step(tt(YT(2)[:, m, :], YT(2)[:, m, :], s_, ALU.mult))
                tt(YT(2)[:, m, :], YT(2)[:, m, :], r_, ALU.mult).then_inc(mixs_taken, 1)

            def onehots(g, q, first=False):
                if not first:
                    v.wait_ge(group_done, g - 1)
                for t in range(GT_):
                    e = g * 8 + t
                    v.tensor_scalar(onehot[:, q, t, 1, :], iota, srcf[:, bass.ds(e, 1)], wts[:, bass.ds(e, 1)],
                                    ALU.is_equal, ALU.mult)
                    v.tensor_scalar(onehot[:, q, t, 0, :], iota, srcf[:, bass.ds(e, 1)], None, ALU.is_equal)
                    v.tensor_scalar(onehot[:, q, t, 2, :], iota, dstf[:, bass.ds(e, 1)], None,
                                    ALU.is_equal).then_inc(oh_ready, 1)

            def take(g, half):
                v.wait_ge(codes_ready, g + 1)
                v.wait_ge(codes_taken, 3 * g + 3)
                for b in range(NB):
                    tt(M[:, half, b, :], bank[2 + b][:, 0:N], M[:, half, b, :], ALU.max).then_inc(codes_taken, 1)

            v.wait_ge(mixs_taken, 8)
            onehots(0, 0, True)
            onehots(1, 1, True)
            take(0, 0)
            take(1, 0)
            with v.Fori(1, EG // 4) as i:
                for q in range(2):
                    onehots(2 * i + q, q)
                take(2 * i, 0)
                take(2 * i + 1, 0)
            with v.Fori(EG // 4, EG // 2) as i:
                for q in range(2):
                    onehots(2 * i + q, q)
                take(2 * i, 1)
                take(2 * i + 1, 1)

            W9 = NB * N
            code = G[:, 0:W9]
            diag = G[:, W9:2 * W9]
            here = G[:, 2 * W9:3 * W9]
            idx = G[:, 3 * W9:4 * W9]
            pick = G[:, 4 * W9:5 * W9]
            mk = mask[:].rearrange("p b n -> p (b n)")
            M1 = Y[:, 1, 0:W9]
            M2 = Y[:, 1, W9:2 * W9]
            v.wait_ge(group_done, EG)
            v.wait_ge(codes_taken, 3 * EG + 3)
            step(stt(code, M2, 0.0, M1, ALU.is_equal, ALU.mult))
            tt(code, code, M2, ALU.add).then_inc(m_taken, 1)
            step(v.memset(diag, 0.0))
            for b in range(NB):
                last = v.tensor_copy(diag[:, b * N + b * P:b * N + (b + 1) * P], ident)
            step(last)
            v.wait_ge(m_taken, 1)
            step(stt(diag, code, 0.0, diag, ALU.is_equal, ALU.mult))
            step(ts(idx.bitcast(I32), code.bitcast(I32), 21, 3, ALU.logical_shift_right, ALU.bitwise_and))
            step(v.tensor_copy(pick, idx.bitcast(I32)))
            step(stt(idx, diag, 3.0, pick, ALU.mult, ALU.add))
            step(stt(here, code, 0.0, diag, ALU.is_gt, ALU.add))
            for c in range(4):
                wc = spw[:, 0, c:c + 1]
                if c == 0:
                    step(ts(mk, idx, 0.0, wc, ALU.is_equal, ALU.mult))
                else:
                    step(ts(pick, idx, float(c), wc, ALU.is_equal, ALU.mult))
                    step(tt(mk, mk, pick, ALU.add))
            step(tt(mk, mk, here, ALU.mult))
            step(ts(here, here, -1.0, -NEG, ALU.add, ALU.mult))
            tt(mk, mk, here, ALU.add).then_inc(mask_ready, 1)
            v.wait_ge(mask_ready, 1)

            def read_scores(h, u, ahead):
                for b in range(NB):
                    v.wait_ge(scores_ready, 3 * h + b + 1)
                    if b == 0 and ahead:
                        v.wait_ge(pt_ready, 3 * h - 9)
                    v.memset(tick[:, 3 * u + b:3 * u + b + 1], 0.0)
                    v.tensor_tensor_reduce(out=S[:, u, b, :], in0=bank[2 + b][:, 0:N], in1=mask[:, b, :], scale=-1.0,
                                           scalar=3e38, op0=ALU.add, op1=ALU.min,
                                           accum_out=nmx[:, u, b:b + 1]).then_inc(scores_read, 1)

            def turn_out(h, first=False):
                v.wait_ge(pt_ready, 3 * h + 3)
                if not first:
                    v.wait_ge(av_ready, h)
                v.tensor_copy(PT[:, 2, :], bank[7][:, 0:N]).then_inc(pt2, 1)

            def take_av(h, u):
                v.wait_ge(exp_done, 3 * h + 3)
                step(v.reciprocal(rinv[:, u, :], rsum[:, u, :]))
                v.wait_ge(av_ready, h + 1)
                dst = xn[:, :, bass.ds(h * DH, DH)]
                tt(dst, bank[u % 2][:, 0:NB * DH].rearrange("p (b d) -> p b d", b=NB),
                   rinv[:, u, :].unsqueeze(2).to_broadcast([P, NB, DH]), ALU.mult).then_inc(av_taken, 1)

            v.wait_ge(t_evicted, T_A)
            read_scores(0, 0, False)
            read_scores(1, 1, False)
            for u in range(4):
                turn_out(u, u == 0)
                read_scores(u + 2, (u + 2) % 4, u >= 2)
                take_av(u, u)
            with v.Fori(1, 3) as i:
                step.enter(i - 1, 4)
                for u in range(4):
                    turn_out(4 * i + u)
                    read_scores(4 * i + u + 2, (u + 2) % 4, True)
                    take_av(4 * i + u, u)
                step.leave(2)
            for u in range(4):
                turn_out(12 + u)
                if u < 2:
                    read_scores(14 + u, u + 2, True)
                take_av(12 + u, u)

            v.wait_ge(bias_added, NB)
            for half in range(2):
                v.wait_ge(chunk_used, CH_O + 8 * half + 8)
                for b in range(NB):
                    d = xr[:, b, half * 512:(half + 1) * 512]
                    tt(d, d, bank[2 + 3 * half + b][:], ALU.add).then_inc(x1_done, 1)
            rstds(1, xr, lambda b: v.wait_ge(x1_done, 4 + b))
            v.wait_ge(tp_ready, 16)
            normalise(xn, xr, xn_ready)

            def small(a, n):
                return w[:, a:a + n]
            mx24 = small(400, 72)
            pr = small(200, 192)
            pr4 = pr.rearrange("p (b e j) -> p b e j", b=NB, e=NE)
            pr3 = pr.rearrange("p (b j) -> p b j", j=NE)
            m24 = small(480, 24)
            s24 = small(504, 24)
            l24 = small(528, 24)
            lg = small(24, 24)
            lg3 = lg.rearrange("p (b e) -> p b e", b=NB)
            gat = small(72, 24)
            gat3 = gat.rearrange("p (b e) -> p b e", b=NB)
            m1, m2, i1, dlt = small(3, 3), small(6, 3), small(9, 3), small(0, 3)
            eq = small(96, 24)
            eq3 = eq.rearrange("p (b e) -> p b e", b=NB)
            oh1 = small(120, 24).rearrange("p (b e) -> p b e", b=NB)
            oh2 = small(144, 24).rearrange("p (b e) -> p b e", b=NB)

            def bc(t, n=NE):
                return t.unsqueeze(2).to_broadcast([P, NB, n])

            def first_max(l3, mx, dst, i1=i1):
                step(v.tensor_reduce(mx, l3, AX.X, ALU.max))
                step(tt(eq3, l3, bc(mx), ALU.is_equal))
                step(stt(eq, eq, -100.0, k32[:, 514:538], ALU.mult, ALU.add))
                step(v.tensor_reduce(i1, eq3, AX.X, ALU.min))
                step(ts(i1, i1, 100.0, None, ALU.add))
                step(tt(dst, iota8, bc(i1), ALU.is_equal))

            v.wait_ge(mixed_ready, 1)
            step(v.tensor_copy(mx24, bank[2][:, 0:72]))
            mixed = mx24.rearrange("p (b c) -> p b c", b=NB)
            for b in range(NB):
                last = tt(pr4[:, b], mixed[:, b, 0:8].unsqueeze(2).to_broadcast([P, NE, NE]),
                          mixed[:, b, 8:16].unsqueeze(1).to_broadcast([P, NE, NE]), ALU.mult)
            step(last)
            step(v.tensor_reduce(m24, pr3, AX.X, ALU.max))
            tt(pr3, pr3, m24.unsqueeze(2).to_broadcast([P, 24, NE]), ALU.subtract).then_inc(gl_sub, 1)
            v.wait_ge(gl_exp, 1)
            step(v.tensor_reduce(s24, pr3, AX.X, ALU.add))
            for b in range(NB):
                last = tt(pr4[:, b], pr4[:, b], mixed[:, b, 16:24].unsqueeze(1).to_broadcast([P, NE, NE]), ALU.mult)
            step(last)
            step(v.tensor_reduce(l24, pr3, AX.X, ALU.add))
            step(v.reciprocal(s24, s24))
            step(tt(lg, l24, s24, ALU.mult))
            first_max(lg3, m1, oh1)
            step(stt(lg3, oh1, -3e38, lg3, ALU.mult, ALU.add))
            first_max(lg3, m2, oh2)
            tt(dlt, m2, m1, ALU.subtract).then_inc(g2_sub, 1)
            v.wait_ge(g2_exp, 1)
            step(ts(m1, dlt, 1.0, None, ALU.add))
            step(v.reciprocal(m1, m1))
            step(tt(m2, dlt, m1, ALU.mult))
            tt(oh1, oh1, bc(m1), ALU.mult)
            step(tt(oh2, oh2, bc(m2), ALU.mult))
            tt(gat3, oh1, oh2, ALU.add).then_inc(gates_ready, 1)
            v.wait_ge(gt_ready, 1)
            v.tensor_copy(GTr[:], bank[3][0:NE, 0:N]).then_inc(gt_done, 1)

            def hidden(n, b):
                v.wait_ge(sig_done, n)
                step(tt(hpre[:, b, :], sg, bank[0][:, 0:N], ALU.mult))
                tt(hpre[:, b, :], hpre[:, b, :], bank[1][:, 0:N], ALU.mult).then_inc(ag_read, 1)

            def gated(n):
                for b in range(2):
                    g = n * 2 + b
                    gt = G[:, bass.ds(g * N, N)]
                    tt(hid[:, b, :], hpre[:, b, :], gt, ALU.mult).then_inc(hid_ready, 1)

            v.wait_ge(chunk_used, CH_F0 + 2)
            hidden(1, 0)
            v.wait_ge(chunk_used, CH_F0 + 4)
            hidden(2, 1)
            v.wait_ge(ag_read, 2)
            v.wait_ge(t_evicted, T_LN3)
            gated(0)
            with v.Fori(1, HB0 // 2) as i:
                step.enter(i - 1, 2)
                v.wait_ge(hid_ready, 2 * i)
                v.wait_ge(chunk_used, CH_F0 - 2 + 6 * i + 2)
                hidden(2 * i + 1, 0)
                v.wait_ge(chunk_used, CH_F0 - 2 + 6 * i + 5)
                hidden(2 * i + 2, 1)
                v.wait_ge(ag_read, 2 * i + 2)
                v.wait_ge(chunk_used, CH_F0 - 2 + 6 * i + 6)
                gated(i)
                step.leave(HB0 // 2 - 1)
            for n in range(6):
                half, b = n // NB, n % NB
                v.wait_ge(acc_ready, n + 1)
                d = xr[:, b, half * 512:(half + 1) * 512]
                tt(d, d, bank[2 + n][:], ALU.add).then_inc(x2_done, 1)
            rstds(2, xr, lambda b: v.wait_ge(x2_done, 4 + b))
            normalise(xn, xr, xn_ready)

            v.wait_ge(l1_in, 16)
            v.wait_ge(h_done, 6)
            h = YN(0)
            for b in range(NB):
                step(v.tensor_tensor_reduce(out=prod, in0=h[:, b, :], in1=a_l, scale=1.0, scalar=0.0,
                                            op0=ALU.mult, op1=ALU.add, accum_out=al[:, b:b + 1]))
                step(v.tensor_tensor_reduce(out=prod, in0=h[:, b, :], in1=a_r, scale=1.0, scalar=0.0,
                                            op0=ALU.mult, op1=ALU.add, accum_out=ar[:, b:b + 1]))
            for b in range(NB):
                last = ts(dg[:, b, :], ident, al[:, b:b + 1], None, ALU.mult)
            last.then_inc(diag_ready, 1)
            v.wait_ge(albc_ready, 1)
            for b in range(NB):
                last = ts(CET[:, b, :], bank[0][:, 0:N], ar[:, b:b + 1], -1.0, ALU.add, ALU.mult)
            step(last)
            stt(eT[:], CET[:], 0.1, CET[:], ALU.mult, ALU.min).then_inc(z_ready, 1)
            v.wait_ge(e_ready, 1)
            tt(CET[:], CT[:], eT[:], ALU.mult).then_inc(cet_ready, 1)
            v.wait_ge(rows2_in, 32)
            for b in range(NB):
                last = tt(xr[:, b, :], xr[:, b, :], rows[:, 1, :], ALU.add)
            step(last)
            v.wait_ge(agg_ready, 1)
            step(ts(rsm, bank[1][:, 0:NB], 1e-5, None, ALU.add))
            step(v.reciprocal(rsi, rsm))
            t_ = YN(4)
            for b in range(NB):
                v.wait_ge(agg_ready, b + 1)
                ts(t_[:, b, 0:512], bank[2 + b][:], rsi[:, b:b + 1], None, ALU.mult)
                ts(t_[:, b, 512:1024], bank[5 + b][:], rsi[:, b:b + 1], None, ALU.mult).then_inc(agg_taken, 1)
            v.wait_ge(agg_taken, NB)
            ts(Y[:, 5, :], Y[:, 4, :], 0.0, None, ALU.min).then_inc(elu_min, 1)
            v.wait_ge(elu_exp, 1)
            xf = xr[:].rearrange("p b d -> p (b d)")
            step(stt(xf, Y[:, 4, :], 0.0, xf, ALU.max, ALU.add))
            step(stt(xf, Y[:, 5, :], -1.0, xf, ALU.add, ALU.add))

            for a in range(8):
                v.wait_ge(kv_ready, a + 1)
                tt(kvbd[:, a, :], bank[a % 2][:, 0:130], bdx, ALU.mult).then_inc(kv_taken, 1)
            for a in range(8):
                v.wait_ge(num_ready, a + 1)
                if a:
                    v.wait_ge(num_taken, a)
                nd = bank[a % 2][:, 0:390].rearrange("p (b c) -> p b c", b=NB)
                step(ts(den[:], nd[:, :, 128:130], 1e-8, None, ALU.add))
                step(v.reciprocal(rden[:], den[:]))
                for j in range(2):
                    last = tt(YN(2)[:, :, a * P + j * DH:a * P + (j + 1) * DH], nd[:, :, j * DH:(j + 1) * DH],
                              rden[:, :, j:j + 1].to_broadcast([P, NB, DH]), ALU.mult)
                last.then_inc(num_taken, 1)
            for half in range(2):
                v.wait_ge(chunk_used, CH_L1 + 32 + 4 * half + 4)
                for b in range(NB):
                    sl = slice(half * 512, (half + 1) * 512)
                    tt(YN(3)[:, b, sl], bank[2 + 3 * half + b][:], xn[:, b, sl], ALU.add).then_inc(zf_done, 1)
            rstds(3, YN(3), lambda b: v.wait_ge(zf_done, 4 + b))
            z3 = YN(3)
            for b in range(NB):
                step(stt(z3[:, b, :], z3[:, b, :], mv[:, b, 0:1], rows[:, 0, :], ALU.subtract, ALU.mult))
                step(stt(xr[:, b, :], z3[:, b, :], rstd[:, b:b + 1], xr[:, b, :], ALU.mult, ALU.add))
            rstds(4, xr)
            normalise(xn, xr, xn_ready)

            v.wait_ge(xn_ready, 4 * NB)
            rstds(5, xn)
            normalise(YN(0), xn, xh_ready)
            v.wait_ge(aff_ready, 1)
            v.tensor_copy(small(0, 24), bank[2][:, 0:24]).then_inc(aff_copied, 1)
            v.wait_ge(aff_copied, 1)
            aff = small(0, 24).rearrange("p (b e) -> p b e", b=NB)
            first_max(aff, small(204, 3), oh1, small(200, 3))
            v.wait_ge(alpha_done, 1)
            tt(gat, small(120, 24), small(24, 24), ALU.mult).then_inc(gate1_ready, 1)
            v.wait_ge(gt1_ready, 1)
            v.tensor_copy(GTr[:], bank[3][0:NE, 0:N]).then_inc(gt1_done, 1)

            def expert_input(e, first=False):
                for k in range(KB):
                    last = ts(YT(3)[:, k, :], YT(2)[:, k, :], cols[:, bass.ds(8 * e + C_GAM + k, 1)],
                              cols[:, bass.ds(8 * e + C_BET + k, 1)], ALU.mult, ALU.add)
                last.then_inc(he_ready, 1)

            def expert_hidden(e):
                for f in range(FB1):
                    v.wait_ge(t_evicted, 4 * e + T_F1 + f + 1)
                    tt(hid1[:, f, :], rl[:, f % 2, :], Y[:, 4, bass.ds(e * N, N)], ALU.mult).then_inc(hid1_ready, 1)

            v.wait_ge(t_evicted, T_XH + 8)
            expert_input(0)
            v.wait_ge(t_evicted, T_GB1 + NE)
            expert_hidden(0)
            with v.Fori(1, NE) as e:
                v.wait_ge(chunk_used, 8 * e + CH_F1 - 4)
                expert_input(e)
                v.wait_ge(chunk_used, 8 * e + CH_F1)
                expert_hidden(e)
            v.wait_ge(feats_added, NB)
            for n in range(6):
                half, b = n // NB, n % NB
                v.wait_ge(acc_ready, 6 + n + 1)
                d = xr[:, b, half * 512:(half + 1) * 512]
                tt(d, d, bank[2 + n][:], ALU.add).then_inc(y_ready, 1)


def t_chunks(a):
    m = a.shape[1] // P
    return np.ascontiguousarray(a.reshape(KB, P, m, P).transpose(2, 1, 0, 3)).reshape(m, P, 1024)


def n_chunks(a):
    k = a.shape[0] // 256
    return np.ascontiguousarray(a.reshape(k, 2, P, 2, 512).transpose(0, 3, 2, 1, 4)).reshape(k, 2, P, 1024)


def halves(*mats):
    cs = [n_chunks(a) for a in mats]
    return [c[:, h] for h in range(2) for c in cs]


def weight_stream(I):
    parts = [t_chunks(I[n].T) for n in ("L0_mix_Wq", "L0_mix_Wk", "L0_mix_Wv", "L0_gnn_wq", "L0_gnn_wk", "L0_gnn_wv",
                                        "L0_gnn_wiq", "L0_gnn_wik")]
    parts += halves(I["L0_gnn_wiv"].T)
    parts += halves(I["L0_mix_Wo"].T, I["L0_gnn_wo"].T)
    w1 = I["L0_ffn_w1"]
    up_a = t_chunks(w1[:, :F0].reshape(NE * F0, D).T)
    up_g = t_chunks(w1[:, F0:].reshape(NE * F0, D).T)
    down = n_chunks(I["L0_ffn_w2"].transpose(0, 2, 1).reshape(NE * F0, D))
    parts += [up_a[0:1], up_g[0:1], up_a[1:2], up_g[1:2]]
    for i in range(1, HB0 // 2):
        b = 2 * i
        parts += [up_a[b:b + 1], up_g[b:b + 1], down[i - 1, 0:1], up_a[b + 1:b + 2], up_g[b + 1:b + 2],
                  down[i - 1, 1:2]]
    parts += [down[HB0 // 2 - 1]]
    parts += halves(I["L1_gnn_W"])
    parts += [t_chunks(I["L1_mix_W_Q"])]
    parts += halves(I["L1_mix_W_K"]) + halves(I["L1_mix_W_V"]) + halves(I["L1_mix_W_fc"])
    for e in range(NE):
        parts += [t_chunks(I["L1_ffn_w1"][e]), n_chunks(I["L1_ffn_w2"][e]).reshape(4, P, 1024)]
    stream = np.concatenate(parts)
    assert stream.shape[0] == CHUNKS
    return stream


def constants():
    f = np.float32
    part, col = np.arange(P)[:, None], np.arange(P)[None, :]
    ident = (part == col).astype(f)
    bd = (part // DH == col // DH).astype(f)
    headcol = (part // DH == np.arange(2)[None, :]).astype(f)
    later = (col > part).astype(f)
    iota8 = np.tile(np.arange(NE, dtype=f) + 100, (P, NB))
    digit = np.tile(np.ldexp(f(1), 3 * (np.arange(ET) % 48) - 72).astype(f), (P, 1))
    c32 = np.concatenate([ident, bd, headcol, later, np.ones((P, P), f), iota8, digit], 1)
    c16 = np.concatenate([np.tile(np.arange(N), (P, 1)), ident, ident * N], 1).astype(np.float16)
    hidden_row = np.arange(HB0 * P)
    sel0 = (hidden_row[None, :] // F0 == np.arange(NE)[:, None]).astype(f).reshape(NE, HB0, P)
    sel1 = np.repeat(np.eye(NE, dtype=f), P, axis=1).reshape(NE, NE, P)
    return c32, c16, sel0, sel1


def kernel(**inputs):
    import concourse.bacc as bacc
    from concourse.bass_utils import run_bass_kernel_spmd as run

    I = {k: np.asarray(a) for k, a in inputs.items()}
    c32, c16, sel0, sel1 = constants()

    def col(a, m=KB):
        return a.reshape(m, P).T

    cols = np.concatenate(
        [col(I[n]) for n in ("L0_mix_bq", "L0_mix_bk", "L0_mix_bv", "L0_gnn_bq", "L0_gnn_bk", "L0_gnn_bv",
                             "L0_gnn_biq", "L0_gnn_bik", "L0_gnn_biv")]
        + [col(np.repeat(I["L0_mix_beta"], DH)), col(I["L1_ffn_b1"], 32), col(I["L1_ffn_gamma"], 64),
           col(I["L1_ffn_beta"], 64), np.tile(I["L0_gnn_edge_type_weights"], (P, 1))], 1)
    edges = np.stack([I[n].reshape(ET, P).T for n in ("src", "dst", "edge_type_5")], 1)
    arrays = {
        "x": I["x"], "stream": weight_stream(I), "c32": c32, "c16": c16, "cols": cols, "edges": edges,
        "sel0": sel0, "sel1": sel1,
        "wqkv": I["L0_ffn_wqkv"].T.reshape(KB, P, 3 * NE).transpose(1, 0, 2),
        "cent": I["L1_ffn_centroids"].T.reshape(KB, P, NE).transpose(1, 0, 2),
        "bo_g": I["L0_gnn_bo"].reshape(1, D), "bo_m": I["L0_mix_bo"].reshape(1, D),
        "a_lr": I["L1_gnn_a"], "gamma": I["L1_mix_gamma"].reshape(1, D), "beta": I["L1_mix_beta"].reshape(1, D),
        "b2": I["L1_ffn_b2"],
    }
    arrays = {k: np.ascontiguousarray(a) for k, a in arrays.items()}
    nc = bacc.Bacc("TRN2", target_bir_lowering=False, num_devices=1)
    args = [nc.dram_tensor("in_" + k, a.shape, mybir.dt.from_np(a.dtype), kind="ExternalInput").ap()
            for k, a in arrays.items()]
    out = nc.dram_tensor("out", (N, D), F32, kind="ExternalOutput").ap()
    program(nc, *args, out)
    r = run(nc, [{"in_" + k: a for k, a in arrays.items()}], core_ids=[0])
    return r.results[0]["out"]
```

```python
from contextlib import ExitStack

import numpy as np
import concourse.bass as bass
from concourse import mybir

F32 = mybir.dt.float32
F16 = mybir.dt.float16
BF16 = mybir.dt.bfloat16
I32 = mybir.dt.int32
U32 = mybir.dt.uint32
ALU = mybir.AluOpType
ACT = mybir.ActivationFunctionType
AX = mybir.AxisListType

P = 128
N = 384
NB = N // P
D = 1024
KB = D // P
HEADS = 16
DH = D // HEADS
EDGES = 12288
ET = EDGES // P
GT_ = 8
EG = ET // GT_
F0 = 352
NE = 8
F1 = 512
FB1 = F1 // P
SLOTS = 8
EPS = 1e-5
NEG = -1e30

CH_A = 0
CH_B = CH_A + 48
CH_O = CH_B + 24
CH_L1 = CH_O + 16
CH_F1 = CH_L1 + 40
CHUNKS = CH_F1 + 64
UPW = 2 * 2 * F0
CAP = 128
LAST = F0 - 2 * P
ROUNDS = NB - 1

C_BIAS = 0
C_BIV = 64
C_BETA = 72
C_B1 = 80
C_GAM = 112
C_BET = 176
C_EW = 240
NCOLS = 244

T_A = 8
T_B = T_A + 48
T_O = T_B + 16
T_LN2 = T_O + 8
T_LN3 = T_LN2 + 8
T_Q = T_LN3 + 8
T_MIX = T_Q + 8
T_FE = T_MIX + 8

EW, GL, G2, ZE, EL, AF = range(1, 7)
MIXED, ALBC, AFF = range(1, 4)
DIAG, CETS = range(1, 3)


class RouteSems:

    def __init__(self, sem, tag):
        self.assigned = sem(tag + "assigned")
        self.ranked = sem(tag + "ranked")
        self.flagged = sem(tag + "flagged")
        self.slots = sem(tag + "slots")
        self.listed = sem(tag + "listed")
        self.rows_known = sem(tag + "rows_known")
        self.dest_known = sem(tag + "dest_known")
        self.over_slots = sem(tag + "over_slots")
        self.over_listed = sem(tag + "over_listed")
        self.over_known = sem(tag + "over_known")


class PassSems:

    def __init__(self, sem, tag, kind, over):
        self.gathered = sem(tag + "gathered")
        self.weights = over and sem(tag + "weights")
        self.xt_ready = sem(tag + "xt_ready")
        self.xt_done = sem(tag + "xt_done")
        self.up_used = sem(tag + "up_used")
        self.sig_done = kind == 0 and sem(tag + "sig_done")
        self.h_ready = sem(tag + "h_ready")
        self.ht_ready = sem(tag + "ht_ready")
        self.ht_done = sem(tag + "ht_done")
        self.dn_used = sem(tag + "dn_used")
        self.y_done = sem(tag + "y_done")
        self.y_stored = sem(tag + "y_stored")
        self.back = over and sem(tag + "back")
        self.turn = over and sem(tag + "turn")


class Chain:

    def __init__(self, eng, sem):
        self.eng, self.sem, self.n, self.off = eng, sem, 0, 0

    def __call__(self, ins):
        self.n += 1
        ins.then_inc(self.sem, 1)
        self.eng.wait_ge(self.sem, self.off + self.n)

    def enter(self, turn, per):
        self.mark, self.per, self.off = self.n, per, turn * per

    def leave(self, turns):
        assert self.n - self.mark == self.per, (self.n, self.mark)
        self.n, self.off = self.mark + self.per * turns, 0


def program(nc, x, stream, c32, c16, cols_d, edges_d, up0_d, dn0_d, wqkv_d, cent_d,
            bo_g, bo_m, a_lr, gam_d, bet_d, b2_d,
            xs, ys, yo, out):
    with ExitStack() as ctx:
        def sb(name, shape, dt=F32):
            return ctx.enter_context(nc.sbuf_tensor(name, shape, dt))

        def sem(name):
            return ctx.enter_context(nc.semaphore(name))

        ring = sb("ring", [P, SLOTS, 1024])
        xr = sb("xr", [P, NB, D])
        xn = sb("xn", [P, NB, D])
        xnT = sb("xnT", [P, KB, N])
        Y = sb("Y", [P, 6, KB * N])
        G = sb("G", [P, 9216])
        mask = sb("mask", [P, NB, N])
        CT = sb("CT", [P, NB, N])
        rows = sb("rows", [P, 2, D])
        k32 = sb("k32", [P, c32.shape[1]])
        k16 = sb("k16", [P, c16.shape[1]], F16)
        cols = sb("cols", [P, NCOLS])
        scale = sb("scale", [P, 64])
        sbias = sb("sbias", [P, 64])
        ed = sb("ed", [P, 3, ET], I32)
        srcf = sb("srcf", [P, ET])
        dstf = sb("dstf", [P, ET])
        keyf = sb("keyf", [P, ET])
        codef = sb("codef", [P, ET])
        ndup = sb("ndup", [P, ET])
        wts = sb("wts", [P, ET])
        src16 = sb("src16", [P, ET], F16)
        dst16 = sb("dst16", [P, ET], F16)
        zero16 = sb("zero16", [P, 512], BF16)
        wqkv = sb("wqkv", [P, KB, 3 * NE])
        cent = sb("cent", [P, KB, NE])
        idx = sb("idx", [P, 48], U32)
        flag = sb("flag", [P, 2], I32)
        st = sb("st", [P, NB, 12])
        mv = sb("mv", [P, NB, 2])
        ve = sb("ve", [P, NB])
        lnv = sb("lnv", [P, NB])
        rs0 = sb("rs0", [P, NB])
        nwt = sb("nwt", [P, NB])
        rstd = sb("rstd", [P, NB])
        nmx = sb("nmx", [P, 4, NB])
        rsum = sb("rsum", [P, 4, NB])
        rinv = sb("rinv", [P, 4, NB])
        tick = sb("tick", [P, 4 * NB])
        spw = sb("spw", [P, 4, 4])
        al = sb("al", [P, NB])
        ar = sb("ar", [P, NB])
        bank = [ctx.enter_context(nc.psum_tensor(f"bank{i}", [P, 512], F32)) for i in range(8)]

        ident = k32[:, 0:128]
        bdx = k32[:, 128:258]
        bd = k32[:, 128:256]
        later = k32[:, 258:386]
        ones = k32[:, 386:514]
        iota8 = k32[:, 514:538].rearrange("p (b e) -> p b e", b=NB)
        ebase = k32[:, 634:658]
        digit = k32[:, 538:538 + ET]
        iota = k16[:, 0:384]
        id16 = k16[:, 384:512]
        id384 = k16[:, 512:640]
        token = k16[:, 640:643]

        def YT(s):
            return Y[:, s, :].rearrange("p (k n) -> p k n", k=KB)

        def YN(s):
            return Y[:, s, :].rearrange("p (b d) -> p b d", b=NB)

        landed = [sem(f"landed{r}") for r in range(SLOTS)]
        chunk_used = sem("chunk_used")
        x_in = [sem(f"x_in{b}") for b in range(NB)]
        k_in = sem("k_in")
        edge_in = sem("edge_in")
        rows_in = sem("rows_in")
        late_in = sem("late_in")
        up_in = [sem(f"up_in{j}") for j in range(4)]
        dn_in = sem("dn_in")
        dn_last = sem("dn_last")
        xs_stored = sem("xs_stored")
        back_in = [sem(f"back_in{b}") for b in range(NB)]
        R0, R1 = RouteSems(sem, "r0_"), RouteSems(sem, "r1_")
        M0, M1s = PassSems(sem, "m0_", 0, False), PassSems(sem, "m1_", 1, False)
        O0, O1 = PassSems(sem, "o0_", 0, True), PassSems(sem, "o1_", 1, True)
        l1_in = sem("l1_in")
        rows2_in = sem("rows2_in")
        b2_in = sem("b2_in")
        ostep = [sem("o0_step"), sem("o1_step")]
        dstep = sem("dstep")
        astep = sem("astep")
        gstep = sem("gstep")
        var_ready = sem("var_ready")
        rstd_seed = sem("rstd_seed")
        act_input = sem("act_input")
        act_output = sem("act_output")
        pe_output = sem("pe_output")
        pe_input = sem("pe_input")
        xn_ready = sem("xn_ready")
        tp_ready = sem("tp_ready")
        t_evicted = sem("t_evicted")
        beta_exp = sem("beta_exp")
        cols_ready = sem("cols_ready")
        bias_added = sem("bias_added")
        edges_ready = sem("edges_ready")
        keys_ready = sem("keys_ready")
        sp_neg = sem("sp_neg")
        sp_exp = sem("sp_exp")
        sp_one = sem("sp_one")
        sp_ln = sem("sp_ln")
        mixprod = sem("mixprod")
        mixs_ready = sem("mixs_ready")
        mixs_taken = sem("mixs_taken")
        oh_ready = sem("oh_ready")
        codes_ready = sem("codes_ready")
        codes_taken = sem("codes_taken")
        group_done = sem("group_done")
        counts_ready = sem("counts_ready")
        ct_done = sem("ct_done")
        m_taken = sem("m_taken")
        mask_ready = sem("mask_ready")
        v2_done = sem("v2_done")
        staged = sem("staged")
        scores_ready = sem("scores_ready")
        scores_read = sem("scores_read")
        exp_done = sem("exp_done")
        pt_ready = sem("pt_ready")
        pt01 = sem("pt01")
        pt2 = sem("pt2")
        av_ready = sem("av_ready")
        av_taken = sem("av_taken")
        x1_done = sem("x1_done")
        x2_done = sem("x2_done")
        h_done = sem("h_done")
        k_done = sem("k_done")
        agg_ready = sem("agg_ready")
        agg_taken = sem("agg_taken")
        v_done = sem("v_done")
        kv_ready = sem("kv_ready")
        kv_taken = sem("kv_taken")
        num_ready = sem("num_ready")
        num_taken = sem("num_taken")
        zf_done = sem("zf_done")
        xh_ready = sem("xh_ready")
        feats_added = sem("feats_added")
        y_ready = sem("y_ready")
        stored = sem("stored")

        junk = CT[:].rearrange("p b n -> p (b n)").bitcast(BF16)[:, 0:GT_ * P].rearrange("p (t n) -> p t n", t=GT_)
        tmp = [G[:, i * 3072:(i + 1) * 3072] for i in range(3)]
        onehot = G[:, :].bitcast(BF16).rearrange("p (q t k n) -> p q t k n", q=2, t=GT_, k=3)
        M = Y[:, 1, 0:2 * NB * N].rearrange("p (h b n) -> p h b n", h=2, b=NB)
        S = G[:, 0:4 * NB * N].rearrange("p (u b n) -> p u b n", u=4, b=NB)
        PT = G[:, 4608:4608 + NB * N].rearrange("p (b n) -> p b n", b=NB)
        qs = G[:, 5760:5760 + 2 * N].rearrange("p (s n) -> p s n", s=2)
        ks = G[:, 6528:6528 + 2 * N].rearrange("p (s n) -> p s n", s=2)
        XgT = [Y[:, a, o:o + 1024].rearrange("p (k n) -> p k n", k=KB) for a, o in ((0, 0), (2, 1024))]
        Xg = Y[:, 0, 1024:2048]
        Yb = Y[:, 0, 2048:3072]
        sg = Y[:, 1, 1024:1024 + F0]
        hid = Y[:, 1, 1408:1920]
        hT = Y[:, 1, 1920:2432].rearrange("p (f n) -> p f n", f=4)
        ringf = ring[:].rearrange("p r n -> p (r n)")
        dnb = Y[0:LAST, 2, 0:1024]
        dnb_over = G[0:LAST, 8192:9216]
        slot = Y[:, 5, 0:1536].bitcast(F16).rearrange("p (b e n) -> p b e n", b=NB, e=NE)
        back = Y[:, 3:5, :].rearrange("p a (c d) -> p (a c) d", c=NB)
        w = Y[:, 1, :]
        kvbd = G[:, 0:8 * 130].rearrange("p (a c) -> p a c", a=8)
        CET = G[:, 1040:1040 + NB * N].rearrange("p (b n) -> p b n", b=NB)
        eT = G[:, 2304:2304 + NB * N].rearrange("p (b n) -> p b n", b=NB)
        dg = G[:, 3456:3456 + NB * P].rearrange("p (b n) -> p b n", b=NB)
        den = G[:, 3840:3840 + 2 * NB].rearrange("p (b j) -> p b j", b=NB)
        rden = G[:, 3850:3850 + 2 * NB].rearrange("p (b j) -> p b j", b=NB)
        rsm = G[:, 3860:3860 + NB]
        rsi = G[:, 3864:3864 + NB]
        a_l = Y[:, 5, 0:1024]
        a_r = Y[:, 5, 1024:2048]
        prod = Y[:, 5, 2048:3072]
        b2row = Y[:, 5, 2048:3072]

        block = ctx.enter_context(nc.Block())

        @block.sync
        def _(sp):
            for b in range(NB):
                sp.dma_start(xr[:, b, :], x[b * P:(b + 1) * P, :]).then_inc(x_in[b], 16)

            def load(r, c):
                sp.dma_start(ring[:, r, :], stream[c]).then_inc(landed[r], 16)

            for r in range(SLOTS):
                load(r, r)
            with sp.Fori(1, CH_L1 // 8) as g:
                for r in range(SLOTS):
                    sp.wait_ge(chunk_used, 8 * g - 7 + r)
                    load(r, 8 * g + r)

            def load_up(e, j):
                sp.dma_start(ringf[:, j * UPW:(j + 1) * UPW], up0_d[e, j]).then_inc(up_in[j], 16)

            def load_dn(e):
                sp.dma_start(ringf[:, 6144:8192].rearrange("p (k n) -> p k n", k=2),
                             dn0_d[e, 0:2 * P, :].rearrange("(k p) n -> p k n", p=P)).then_inc(dn_in, 16)
                sp.dma_start(dnb, dn0_d[e, 2 * P:F0, :]).then_inc(dn_in, 16)

            for j in range(4):
                sp.wait_ge(chunk_used, CH_L1 - 8 + ((j + 1) * UPW - 1) // 1024 + 1)
                load_up(0, j)
            sp.wait_ge(chunk_used, CH_L1)
            load_dn(0)
            sp.wait_ge(x1_done, 6)
            sp.dma_start(G[:, 6144:8192].rearrange("p (k n) -> p k n", k=2),
                         dn0_d[NE - 1, 0:2 * P, :].rearrange("(k p) n -> p k n", p=P)).then_inc(dn_last, 16)
            sp.dma_start(dnb_over, dn0_d[NE - 1, 2 * P:F0, :]).then_inc(dn_last, 16)

            def next_up(e):
                for j in range(4):
                    sp.wait_ge(M0.up_used, 4 * e - 3 + j)
                    load_up(e, j)

            next_up(1)
            with sp.Fori(2, NE) as e:
                next_up(e)
                sp.wait_ge(M0.dn_used, e - 1)
                load_dn(e - 1)
            sp.wait_ge(M0.up_used, 4 * NE)
            for b in range(NB):
                sp.wait_ge(back_in[b], 32)
            for r in range(6):
                load(r, CH_L1 + r)
            sp.wait_ge(M0.dn_used, NE - 1)
            for r in range(6, 8):
                load(r, CH_L1 + r)
            with sp.Fori(CH_L1 // 8 + 1, CH_F1 // 8 + 1) as g:
                for r in range(SLOTS):
                    sp.wait_ge(chunk_used, 8 * g - 7 + r)
                    load(r, 8 * g + r)
            def next_w1(e):
                for r in range(4):
                    sp.wait_ge(M1s.up_used, 4 * e - 3 + r)
                    load(r, 8 * e + CH_F1 + r)

            def next_w2(e):
                for r in range(4, 8):
                    sp.wait_ge(M1s.dn_used, 4 * e - 7 + r)
                    load(r, 8 * e + CH_F1 + r)

            def load_b2(e):
                sp.dma_start(b2row, b2_d[e].to_broadcast([P, D])).then_inc(b2_in, 16)

            sp.wait_ge(zf_done, 6)
            load_b2(0)
            next_w1(1)
            with sp.Fori(2, NE) as e:
                next_w1(e)
                next_w2(e - 1)
                sp.wait_ge(M1s.y_done, e - 1)
                load_b2(e - 1)
            next_w2(NE - 1)
            sp.wait_ge(M1s.y_done, NE - 1)
            load_b2(NE - 1)
            for b in range(NB):
                sp.wait_ge(y_ready, b + 1)
                sp.dma_start(out[b * P:(b + 1) * P, :], xr[:, b, :]).then_inc(stored, 16)
            sp.wait_ge(stored, 16 * NB)

        @block.gpsimd
        def _(pool):
            step = Chain(pool, gstep)
            pool.wait_ge(rows_in, 32)
            step(pool.tensor_tensor(rows[:, 0, :], rows[:, 0, :], rows[:, 1, :], ALU.add))
            pool.wait_ge(xn_ready, NB)
            for b in range(NB):
                pool.tensor_tensor(xr[:, b, :], xr[:, b, :], rows[:, 0, :], ALU.add).then_inc(bias_added, 1)
            pool.wait_ge(bias_added, NB)
            pool.dma_start(rows[:, 0, :], gam_d.to_broadcast([P, D])).then_inc(rows2_in, 16)
            pool.dma_start(rows[:, 1, :], bet_d.to_broadcast([P, D])).then_inc(rows2_in, 16)
            for p in range(2):
                pool.wait_ge(t_evicted, T_B + 8 + p + 1)
                if p == 0:
                    pool.wait_ge(mask_ready, 1)
                pool.tensor_copy(qs[:, p, :], YT(0)[:, p, :])
                pool.tensor_copy(ks[:, p, :], YT(1)[:, p, :]).then_inc(staged, 1)
            pool.wait_ge(t_evicted, T_O)
            with pool.Fori(1, 4) as i:
                for p in range(2):
                    pool.wait_ge(scores_ready, 12 * i - 12 + 6 * p + 6)
                    pool.tensor_copy(qs[:, p, :], Y[:, 0, bass.ds((2 * i + p) * N, N)])
                    pool.tensor_copy(ks[:, p, :], Y[:, 1, bass.ds((2 * i + p) * N, N)]).then_inc(staged, 1)

            def gather(dst, src, col, done):
                pool.indirect_dma_start(dst, None, src, bass.IndirectOffsetOnAxis(ap=idx[:, col:col + 1], axis=0))\
                    .then_inc(done, 16)

            def experts(R, S, between):
                for e in range(NE):
                    pool.wait_ge(R.rows_known, 1 if e == 0 else 2)
                    if e == 0:
                        pool.wait_ge(xs_stored, 48 if S is M0 else 96)
                    else:
                        pool.wait_ge(S.xt_ready, 2 * e)
                    gather(Xg, xs, e, S.gathered)
                    if e == 0:
                        between()

            def give_back(R, S, choices):
                pool.wait_ge(R.dest_known, 1)
                pool.wait_ge(S.y_stored, 16 * NE)
                for b in range(NB):
                    for c in range(choices):
                        gather(back[:, c * NB + b, :], ys, 8 + c * NB + b, back_in[b])

            def overflow(R, S, kind, choices):
                for v in range(ROUNDS * NE):
                    e = v % NE
                    pool.wait_ge(R.over_known, 1 + v // NE)
                    pool.wait_ge(S.turn, v + 1)
                    if kind == 0:
                        for j in range(4):
                            pool.dma_start(G[:, j * UPW:(j + 1) * UPW], up0_d[e, j]).then_inc(S.weights, 16)
                        pool.dma_start(G[:, 6144:8192].rearrange("p (k n) -> p k n", k=2),
                                       dn0_d[e, 0:2 * P, :].rearrange("(k p) n -> p k n", p=P))\
                            .then_inc(S.weights, 16)
                        pool.dma_start(dnb_over, dn0_d[e, 2 * P:F0, :]).then_inc(S.weights, 16)
                    else:
                        for r in range(SLOTS):
                            pool.dma_start(G[:, r * 1024:(r + 1) * 1024], stream[CH_F1 + 8 * e + r])\
                                .then_inc(S.weights, 16)
                        pool.dma_start(b2row, b2_d[e].to_broadcast([P, D])).then_inc(S.weights, 16)
                    gather(Xg, xs, 16 + v, S.gathered)
                pool.wait_ge(R.over_known, ROUNDS + 1)
                for n in range(choices * NB):
                    pool.wait_ge(S.turn, ROUNDS * NE + n + 1)
                    gather(Xg, yo, 32 + n, S.back)

            def branch(R, layer):
                pool.wait_ge(R.flagged, 1)
                return pool.value_load(flag[0:1, layer:layer + 1])

            experts(R0, M0, lambda: None)
            over0 = branch(R0, 0)
            give_back(R0, M0, 2)
            with pool.If(over0 > 0):
                overflow(R0, O0, 0, 2)
            pool.wait_ge(xn_ready, 3 * NB)
            pool.dma_start(Y[:, 5, 0:2048], a_lr.to_broadcast([P, 2 * D])).then_inc(l1_in, 16)

            def add_feats():
                pool.wait_ge(xh_ready, NB)
                for b in range(NB):
                    pool.tensor_tensor(xr[:, b, :], xr[:, b, :], xn[:, b, :], ALU.add).then_inc(feats_added, 1)

            experts(R1, M1s, add_feats)
            over1 = branch(R1, 1)
            give_back(R1, M1s, 1)
            with pool.If(over1 > 0):
                overflow(R1, O1, 1, 1)

        @block.scalar
        def _(act):
            step = Chain(act, astep)
            act.dma_start(k32[:], c32).then_inc(k_in, 16)
            act.dma_start(ed[:], edges_d).then_inc(edge_in, 16)
            act.dma_start(k16[:], c16).then_inc(k_in, 16)
            act.dma_start(cols[:], cols_d).then_inc(k_in, 16)
            act.dma_start(rows[:, 0, :], bo_g.to_broadcast([P, D])).then_inc(rows_in, 16)
            act.dma_start(rows[:, 1, :], bo_m.to_broadcast([P, D])).then_inc(rows_in, 16)
            act.dma_start(wqkv[:], wqkv_d).then_inc(late_in, 16)
            act.dma_start(cent[:], cent_d).then_inc(late_in, 16)

            def store_rows(src):
                for b in range(NB):
                    act.dma_start(xs[b * P:(b + 1) * P, :], src[:, b, :]).then_inc(xs_stored, 16)

            def seed(c):
                act.wait_ge(var_ready, c + 1)
                step(act.activation(lnv[:], ve[:], ACT.Ln))
                act.activation(rs0[:], lnv[:], ACT.Exp, scale=-0.5).then_inc(rstd_seed, 1)

            def evict_transposes(base, first, dst, bias=None):
                for m in range(KB):
                    act.wait_ge(tp_ready, first + m + 1)
                    b = bank[(base + m) % 2][:, 0:N]
                    if bias is None:
                        act.activation(dst[:, m, :], b, ACT.Copy).then_inc(t_evicted, 1)
                    else:
                        act.activation(dst[:, m, :], b, ACT.Identity,
                                       bias=cols[:, bias + m:bias + m + 1]).then_inc(t_evicted, 1)

            seed(0)
            act.wait_ge(k_in, 48)
            act.activation(scale[:, 0:8], cols[:, C_BETA:C_BETA + 8], ACT.Exp, scale=-1.0).then_inc(beta_exp, 1)
            act.activation(spw[:, 1, :], cols[:, C_EW:C_EW + 4], ACT.Abs)
            step(act.activation(spw[:, 0, :], cols[:, C_EW:C_EW + 4], ACT.Copy))
            act.activation(spw[:, 2, :], spw[:, 1, :], ACT.Exp, scale=-1.0).then_inc(beta_exp, 1)
            act.wait_ge(act_input, EW)
            act.activation(spw[:, 1, :], spw[:, 3, :], ACT.Ln).then_inc(act_output, 1)
            evict_transposes(0, 0, xnT)

            def evict_T(layer, m):
                if isinstance(layer, int):
                    dst = Y[:, layer, m * N:(m + 1) * N]
                    sc = scale[:, layer * 8 + m:layer * 8 + m + 1]
                    bi = sbias[:, layer * 8 + m:layer * 8 + m + 1]
                else:
                    dst = Y[:, bass.ds(layer, 1), m * N:(m + 1) * N].rearrange("p a n -> p (a n)")
                    sc = scale[:, bass.ds(layer * 8 + m, 1)]
                    bi = sbias[:, bass.ds(layer * 8 + m, 1)]
                act.wait_ge(chunk_used, layer * 8 + m + 1)
                act.activation(dst, bank[m % 2][:, 0:N], ACT.Identity, bias=bi, scale=sc).then_inc(t_evicted, 1)

            act.wait_ge(cols_ready, 1)
            for m in range(KB):
                evict_T(0, m)
            with act.Fori(0, 2) as s:
                for m in range(3):
                    evict_T(s + 1, m)
                act.wait_ge(sp_neg, s + 1)
                act.activation(tmp[1], tmp[0], ACT.Exp).then_inc(sp_exp, 1)
                for m in range(3, 6):
                    evict_T(s + 1, m)
                act.wait_ge(sp_one, s + 1)
                act.activation(tmp[2], tmp[0], ACT.Ln).then_inc(sp_ln, 1)
                for m in range(6, 8):
                    evict_T(s + 1, m)
            with act.Fori(3, 6) as layer:
                for m in range(KB):
                    evict_T(layer, m)

            act.wait_ge(counts_ready, 1)
            for b in range(NB):
                act.activation(CT[:, b, :], bank[5 + b][:, 0:N], ACT.Copy).then_inc(ct_done, 1)

            act.wait_ge(mixs_taken, 8)
            act.wait_ge(m_taken, 1)
            with act.Fori(0, 2) as j:
                for m in range(KB):
                    act.wait_ge(chunk_used, CH_B + 8 * j + m + 1)
                    act.activation(Y[:, bass.ds(j, 1), m * N:(m + 1) * N].rearrange("p a n -> p (a n)"),
                                   bank[m % 2][:, 0:N], ACT.Identity,
                                   bias=sbias[:, bass.ds(j * 8 + 48 + m, 1)],
                                   scale=scale[:, bass.ds(j * 8 + 48 + m, 1)]).then_inc(t_evicted, 1)

            def evict_N(base, dst, func, done):
                for half in range(2):
                    act.wait_ge(chunk_used, base + 4 * half + 4)
                    for b in range(NB):
                        act.activation(dst[:, b, half * 512:(half + 1) * 512],
                                       bank[2 + 3 * half + b][:], func).then_inc(done, 1)

            evict_N(CH_B + 16, YN(3), ACT.Copy, v2_done)

            def exps(h, u):
                for b in range(NB):
                    act.wait_ge(scores_read, 3 * h + b + 1)
                    act.activation(S[:, u, b, :], S[:, u, b, :], ACT.Exp, scale=-1.0, bias=nmx[:, u, b:b + 1],
                                   accum_out=rsum[:, u, b:b + 1]).then_inc(exp_done, 1)

            def turn_out(h, first=False):
                for mb in range(2):
                    act.wait_ge(pt_ready, 3 * h + mb + 1)
                    if mb == 0 and not first:
                        act.wait_ge(av_ready, h)
                    act.activation(PT[:, mb, :], bank[5 + mb][:, 0:N], ACT.Copy).then_inc(pt01, 1)

            exps(0, 0)
            exps(1, 1)
            for u in range(4):
                turn_out(u, u == 0)
                exps(u + 2, (u + 2) % 4)
            with act.Fori(1, 3) as i:
                for u in range(4):
                    turn_out(4 * i + u)
                    exps(4 * i + u + 2, (u + 2) % 4)
            for u in range(4):
                turn_out(12 + u)
                if u < 2:
                    exps(14 + u, u + 2)

            evict_transposes(T_O, 8, YT(4), bias=C_BIV)
            seed(1)
            act.wait_ge(xn_ready, 2 * NB)
            store_rows(xn)
            evict_transposes(T_LN2, 16, xnT)

            act.wait_ge(act_input, GL)
            act.activation(w[:, 200:392], w[:, 200:392], ACT.Exp).then_inc(act_output, 1)
            act.wait_ge(act_input, G2)
            act.activation(w[:, 0:3], w[:, 0:3], ACT.Exp).then_inc(act_output, 1)

            def rows_T(S, v, kind, e, buf=0):
                for i in range(2):
                    act.wait_ge(S.xt_ready, 2 * v + i + 1)
                    if kind == 0:
                        last = act.activation(XgT[buf][:, 4 * i:4 * i + 4, :].rearrange("p k n -> p (k n)"),
                                              bank[i][:], ACT.Copy)
                    else:
                        for k in range(4):
                            g = 8 * e + 4 * i + k
                            last = act.activation(XgT[buf][:, 4 * i + k, :], bank[i][:, k * P:(k + 1) * P], ACT.Identity,
                                                  scale=cols[:, bass.ds(g + C_GAM, 1)],
                                                  bias=cols[:, bass.ds(g + C_BET, 1)])
                    last.then_inc(S.xt_done, 1)

            def act_hidden(S, v, kind, e):
                if kind == 0:
                    act.wait_ge(S.up_used, 4 * v + 4)
                    act.activation(sg, bank[2][:, 0:F0], ACT.Sigmoid).then_inc(S.sig_done, 1)
                else:
                    act.wait_ge(S.ht_ready, v + 1)
                    for f in range(FB1):
                        last = act.activation(hT[:, f, :], bank[4][:, f * P:(f + 1) * P], ACT.Relu,
                                              bias=cols[:, bass.ds(4 * e + C_B1 + f, 1)])
                    last.then_inc(S.ht_done, 1)

            def output(S, v, kind, rows_out, free):
                if kind == 0:
                    act.wait_ge(S.dn_used, v + 1)
                    if free:
                        act.wait_ge(S.y_stored, 16 * v)
                    for half in range(2):
                        last = act.activation(Yb[:, half * 512:(half + 1) * 512], bank[5 + half][:], ACT.Copy)
                    last.then_inc(S.y_done, 1)
                act.wait_ge(S.y_done, v + 1)
                act.dma_start(rows_out[bass.ds(v * CAP, CAP), :], Yb).then_inc(S.y_stored, 16)

            def act_experts(S, kind):
                def turn(e, q, free=True, last=False):
                    if not last:
                        rows_T(S, e + 1, kind, e + 1, 1 - q)
                    if kind == 0:
                        act_hidden(S, e, kind, e)
                    output(S, e - 1, kind, ys, free)
                    if kind == 1:
                        act_hidden(S, e, kind, e)

                rows_T(S, 0, kind, 0, 0)
                if kind == 0:
                    act_hidden(S, 0, kind, 0)
                rows_T(S, 1, kind, 1, 1)
                if kind == 0:
                    act_hidden(S, 1, kind, 1)
                    rows_T(S, 2, kind, 2, 0)
                    output(S, 0, kind, ys, False)
                else:
                    act_hidden(S, 0, kind, 0)
                    turn(1, 1, False)
                with act.Fori(1, NE // 2 - 1) as i:
                    for q in range(2):
                        turn(2 * i + q, q)
                turn(NE - 2, 0)
                turn(NE - 1, 1, last=True)
                output(S, NE - 1, kind, ys, True)

            def act_overflow(R, S, kind, layer):
                act.wait_ge(R.flagged, 1)
                over = act.value_load(flag[0:1, layer:layer + 1])
                with act.If(over > 0):
                    with act.Fori(0, ROUNDS) as r:
                        with act.Fori(0, NE) as e:
                            v = 8 * r + e
                            rows_T(S, v, kind, e)
                            act_hidden(S, v, kind, e)
                            output(S, v, kind, yo, False)

            act_experts(M0, 0)
            act_overflow(R0, O0, 0, 0)
            seed(2)
            evict_transposes(T_LN3, 24, xnT)
            evict_N(CH_L1, YN(0), ACT.Copy, h_done)
            for m in range(KB):
                act.wait_ge(chunk_used, CH_L1 + 8 + m + 1)
                act.activation(YT(1)[:, m, :], bank[m % 2][:, 0:N], ACT.Sigmoid).then_inc(t_evicted, 1)
            act.wait_ge(act_input, ZE)
            act.activation(eT[:], eT[:], ACT.Exp).then_inc(act_output, 1)
            evict_N(CH_L1 + 16, YN(2), ACT.Sigmoid, k_done)
            act.wait_ge(act_input, EL)
            act.activation(Y[:, 5, :], Y[:, 5, :], ACT.Exp).then_inc(act_output, 1)
            evict_N(CH_L1 + 24, YN(3), ACT.Copy, v_done)
            act.wait_ge(kv_taken, 8)
            evict_transposes(T_MIX, 32, YT(1))
            seed(3)
            seed(4)
            evict_transposes(T_FE, 40, xnT)
            seed(5)
            act.wait_ge(act_input, AF)
            act.activation(w[:, 24:48], w[:, 216:240], ACT.Sigmoid).then_inc(act_output, 1)
            act.wait_ge(xh_ready, NB)
            store_rows(YN(2))
            act_experts(M1s, 1)
            act_overflow(R1, O1, 1, 1)

        @block.tensor
        def _(pe):
            def transposes(base, src, dst_blocks=KB):
                for m in range(KB):
                    n = base + m
                    if n >= 2:
                        pe.wait_ge(t_evicted, n - 1)
                    for b in range(NB):
                        last = pe.transpose(bank[n % 2][:, b * P:(b + 1) * P], src[:, b, m * P:(m + 1) * P], ident)
                    last.then_inc(tp_ready, 1)

            def chunk_T(r, rhs, free, arrived, to):
                pe.wait_ge(landed[r], arrived)
                pe.wait_ge(t_evicted, free)
                for k in range(KB):
                    last = pe.matmul(bank[to][:, 0:N], ring[:, r, k * P:(k + 1) * P], rhs(k),
                                     start=(k == 0), stop=(k == KB - 1))
                last.then_inc(chunk_used, 1)

            def chunk_N(r, lhs, k0, half, arrived, start, stop):
                pe.wait_ge(landed[r], arrived)
                for k in range(2):
                    for b in range(NB):
                        last = pe.matmul(bank[2 + 3 * half + b][:], lhs(k0 + k, b),
                                         ring[:, r, k * 512:(k + 1) * 512],
                                         start=(start and k == 0), stop=(stop and k == 1), skip_group_check=True)
                last.then_inc(chunk_used, 1)

            def layer_N(g, lhs, arrived, wait_half):
                for half in range(2):
                    wait_half(half)
                    for kk in range(4):
                        r = 4 * half + kk
                        chunk_N(r, lhs, 2 * kk, half, arrived(r), kk == 0, kk == 3)

            def tok(area):
                v = YT(area)
                return lambda k, b: v[:, k, b * P:(b + 1) * P]

            def xtok(k, b):
                return xnT[:, k, b * P:(b + 1) * P]

            pe.wait_ge(k_in, 48)
            pe.wait_ge(xn_ready, NB)
            transposes(0, xn)
            pe.wait_ge(t_evicted, T_A)

            def keys(layer):
                pe.wait_ge(edges_ready, 2 * layer + 2)
                for g in range(2):
                    for t in range(GT_):
                        dst = bank[4 + 2 * g + t // 4][:, (t % 4) * P:(t % 4 + 1) * P]
                        e = layer * 16 + g * 8 + t
                        pe.matmul(dst, src16[:, bass.ds(e, 1)].to_broadcast([P, P]), id384, start=True, stop=False)
                        last = pe.matmul(dst, dst16[:, bass.ds(e, 1)].to_broadcast([P, P]), id16,
                                         start=False, stop=True)
                    last.then_inc(keys_ready, 1)

            def layer_A(layer, before=None):
                keys(layer)
                for m in range(KB):
                    if before:
                        before(m)
                    chunk_T(m, lambda k: xnT[:, k, :], layer * 8 + m + T_A - 1, layer * 16 + 16, m % 2)

            with pe.Fori(0, 5) as layer:
                layer_A(layer)

            def head_sums(m):
                if m == 0:
                    pe.wait_ge(mixprod, 1)
                if m >= 2:
                    pe.wait_ge(mixs_taken, m - 1)
                pe.matmul(bank[2 + m % 2][:, 0:N], bd, YT(0)[:, m, :], start=True, stop=True).then_inc(mixs_ready, 1)

            layer_A(5, head_sums)

            pe.wait_ge(mixs_taken, 8)
            pe.wait_ge(edges_ready, 2 + EG)
            for b in range(NB):
                pe.matmul(bank[5 + b][:, 0:N], zero16[:, 0:P], zero16[:, 0:N], start=True, stop=False,
                          skip_group_check=True)
            with pe.Fori(0, EG // 2) as i:
                for q in range(2):
                    g = 2 * i + q
                    pe.wait_ge(codes_taken, 3 * g + 3)
                    for t in range(GT_):
                        pe.wait_ge(oh_ready, 8 * g + t + 1)
                        for b in range(NB):
                            last = pe.matmul(bank[2 + b][:, 0:N], onehot[:, q, t, 1, b * P:(b + 1) * P],
                                             onehot[:, q, t, 2, :], start=(t == 0), stop=(t == GT_ - 1),
                                             skip_group_check=True)
                    last.then_inc(codes_ready, 1)
                    for t in range(GT_):
                        for b in range(NB):
                            last = pe.matmul(bank[5 + b][:, 0:N], onehot[:, q, t, 2, b * P:(b + 1) * P],
                                             onehot[:, q, t, 0, :], start=False, stop=False, skip_group_check=True)
                    last.then_inc(group_done, 1)
            for b in range(NB):
                last = pe.matmul(bank[5 + b][:, 0:N], zero16[:, 0:P], zero16[:, 0:N], start=False, stop=True,
                                 skip_group_check=True)
            last.then_inc(counts_ready, 1)

            with pe.Fori(0, 2) as j:
                for m in range(KB):
                    chunk_T(m, lambda k: Y[:, bass.ds(j + 3, 1), k * N:(k + 1) * N].rearrange("p a n -> p (a n)"),
                            8 * j + m + T_B - 1, 16 * j + 16 * (CH_B // 8 + 1), m % 2)

            def free_b(half):
                if half == 0:
                    pe.wait_ge(codes_taken, 3 * EG + 3)
                else:
                    pe.wait_ge(ct_done, NB)
            layer_N(0, tok(5), lambda r: 16 * (CH_B // 8 + 3), free_b)

            def scores(h, u, first=False):
                o = 64 * (u % 2)
                for b in range(NB):
                    if not first:
                        pe.wait_ge(scores_read, 3 * h - 3 + b + 1)
                    last = pe.matmul(bank[2 + b][:, 0:N], qs[o:o + 64, u // 2, b * P:(b + 1) * P],
                                     ks[o:o + 64, u // 2, :], start=True, stop=True).then_inc(scores_ready, 1)

            def turn(h, u, first=False):
                pe.wait_ge(exp_done, 3 * h + 3)
                for mb in range(NB):
                    if not first:
                        if mb < 2:
                            pe.wait_ge(pt01, 2 * h - 2 + mb + 1)
                        else:
                            pe.wait_ge(pt2, h)
                    for b in range(NB):
                        last = pe.transpose(bank[5 + mb][:, b * P:(b + 1) * P], S[:, u, b, mb * P:(mb + 1) * P], ident)
                    last.then_inc(pt_ready, 1)

            def weigh(h, u, first=False):
                pe.wait_ge(pt01, 2 * h + 2)
                pe.wait_ge(pt2, h + 1)
                if not first:
                    pe.wait_ge(av_taken, h - 1)
                for b in range(NB):
                    for mb in range(NB):
                        last = pe.matmul(bank[u % 2][:, b * DH:(b + 1) * DH], PT[:, mb, b * P:(b + 1) * P],
                                         Y[:, 3, bass.ds(h * DH + mb * D, DH)], start=(mb == 0), stop=(mb == NB - 1))
                last.then_inc(av_ready, 1)

            pe.wait_ge(v2_done, 6)
            pe.wait_ge(t_evicted, T_O)
            pe.wait_ge(staged, 1)
            scores(0, 0, True)
            scores(1, 1)
            for u in range(4):
                turn(u, u, u == 0)
                if u == 0 or u == 2:
                    pe.wait_ge(staged, u // 2 + 2)
                scores(u + 2, (u + 2) % 4)
                weigh(u, u, u < 2)
            with pe.Fori(1, 3) as i:
                for u in range(4):
                    turn(4 * i + u, u)
                    if u == 0 or u == 2:
                        pe.wait_ge(staged, 2 * i + u // 2 + 2)
                    scores(4 * i + u + 2, (u + 2) % 4)
                    weigh(4 * i + u, u)
            for u in range(4):
                turn(12 + u, u)
                if u == 0:
                    pe.wait_ge(staged, 8)
                if u < 2:
                    scores(14 + u, u + 2)
                weigh(12 + u, u)

            pe.wait_ge(scores_read, 48)
            for kk in range(4):
                chunk_N(kk, tok(2), 2 * kk, 0, 16 * (CH_O // 8 + 1), kk == 0, False)
            pe.wait_ge(av_taken, HEADS)
            transposes(T_O, xn)
            pe.wait_ge(t_evicted, T_O + 8)
            for kk in range(4):
                chunk_N(4 + kk, tok(4), 2 * kk, 0, 16 * (CH_O // 8 + 1), False, kk == 3)
            pe.wait_ge(pt01, 32)
            pe.wait_ge(pt2, 16)
            for kk in range(4):
                chunk_N(kk, tok(2), 2 * kk, 1, 16 * (CH_O // 8 + 2), kk == 0, False)
            for kk in range(4):
                chunk_N(4 + kk, tok(4), 2 * kk, 1, 16 * (CH_O // 8 + 2), False, kk == 3)

            pe.wait_ge(xn_ready, 2 * NB)
            transposes(T_LN2, xn)
            pe.wait_ge(late_in, 32)
            pe.wait_ge(t_evicted, T_LN2 + 8)
            for b in range(NB):
                for k in range(KB):
                    last = pe.matmul(bank[2][:, b * 24:(b + 1) * 24], xtok(k, b), wqkv[:, k, :],
                                     start=(k == 0), stop=(k == KB - 1))
            last.then_inc(pe_output, 1)

            def route(R):
                A = w[:, 168:192].rearrange("p (b e) -> p b e", b=NB)
                pe.wait_ge(R.assigned, 1)
                for b in range(NB):
                    for a in range(b + 1):
                        pe.matmul(bank[2][:, 96 + b * 8:96 + b * 8 + 8], later if a == b else ones, A[:, a, :],
                                  start=(a == 0), stop=(a == b))
                for a in range(NB):
                    last = pe.matmul(bank[2][:, 120:128], ones, A[:, a, :], start=(a == 0), stop=(a == NB - 1))
                last.then_inc(R.ranked, 1)
                for e in range(NE):
                    pe.wait_ge(R.slots, e + 1)
                    for b in range(NB):
                        last = pe.matmul(bank[3 if e == 0 else 4][:, e:e + 1], slot[:, b, e, :], token[:, b:b + 1],
                                         start=(b == 0), stop=(b == NB - 1))
                    if e == 0 or e == NE - 1:
                        last.then_inc(R.listed, 1)

            def turn_rows(S, v, first=False):
                pe.wait_ge(S.gathered, 16 * v + 16)
                if not first:
                    pe.wait_ge(S.xt_done, 2 * v)
                for i in range(2):
                    for k in range(4):
                        last = pe.transpose(bank[i][:, k * P:(k + 1) * P], Xg[:, (4 * i + k) * P:(4 * i + k + 1) * P],
                                            ident)
                    last.then_inc(S.xt_ready, 1)

            def up(S, v, kind, W, arrived, buf=0):
                pe.wait_ge(S.xt_done, 2 * v + 2)
                for j in range(4):
                    arrived(j)
                    for k in range(2):
                        x_ = XgT[buf][:, 2 * j + k, :]
                        se = dict(start=(j == 0 and k == 0), stop=(j == 3 and k == 1))
                        if kind == 0:
                            for h in range(2):
                                o = j * UPW + (2 * k + h) * F0
                                last = pe.matmul(bank[2 + h][:, 0:F0], x_, W[:, o:o + F0], **se)
                        else:
                            o = j * 1024 + k * 512
                            last = pe.matmul(bank[2][:], x_, W[:, o:o + 512], **se)
                    last.then_inc(S.up_used, 1)

            def turn_hidden(S, v, kind):
                pe.wait_ge(S.h_ready, v + 1)
                for f in range(3 if kind == 0 else 4):
                    n = LAST if kind == 0 and f == 2 else P
                    last = pe.transpose(bank[4][0:n, f * P:(f + 1) * P], hid[:, f * P:f * P + n], ident)
                last.then_inc(S.ht_ready, 1)

            def down(S, v, kind, W, Wb, arrived, free):
                pe.wait_ge(S.ht_done, v + 1)
                if free:
                    pe.wait_ge(S.y_done, v)
                arrived(0)
                if kind == 0:
                    for half in range(2):
                        for f in range(3):
                            h_ = hT[0:LAST, f, :] if f == 2 else hT[:, f, :]
                            w_ = (Wb[:, half * 512:(half + 1) * 512] if f == 2 else
                                  W[:, 6144 + f * 1024 + half * 512:6144 + f * 1024 + (half + 1) * 512])
                            last = pe.matmul(bank[5 + half][:], h_, w_, start=(f == 0), stop=(f == 2))
                    last.then_inc(S.dn_used, 1)

            pe.wait_ge(t_evicted, T_LN2 + 8)
            route(R0)

            def up_arrived0(e):
                return lambda j: pe.wait_ge(up_in[j], 16 * e + 16)

            def dn_arrived0(e):
                return lambda j: pe.wait_ge(dn_in, 32 * e + 32)

            def pe_experts(S, R, up_, down_):
                kind = 0 if S is M0 else 1

                def turn(e, q):
                    turn_rows(S, e + 1)
                    up_(e, q)
                    down_(e - 1)
                    turn_hidden(S, e, kind)

                turn_rows(S, 0, True)
                pe.wait_ge(R.rows_known, 2)
                up_(0, 0)
                turn_rows(S, 1)
                turn_hidden(S, 0, kind)
                up_(1, 1)
                turn_rows(S, 2)
                down_(0)
                turn_hidden(S, 1, kind)
                with pe.Fori(1, NE // 2 - 1) as i:
                    for q in range(2):
                        turn(2 * i + q, q)
                turn(NE - 2, 0)
                up_(NE - 1, 1)
                down_(NE - 2)
                turn_hidden(S, NE - 1, kind)
                down_(NE - 1)

            def down0(e):
                if isinstance(e, int) and e == NE - 1:
                    down(M0, e, 0, G, dnb_over, lambda j: pe.wait_ge(dn_last, 32), True)
                else:
                    down(M0, e, 0, ringf, dnb, dn_arrived0(e), not isinstance(e, int) or e > 0)

            pe_experts(M0, R0, lambda e, b: up(M0, e, 0, ringf, up_arrived0(e), b), down0)

            def pe_overflow(R, S, kind, layer):
                pe.wait_ge(R.flagged, 1)
                over = pe.value_load(flag[0:1, layer:layer + 1])
                with pe.If(over > 0):
                    for r in range(ROUNDS):
                        pe.wait_ge(R.over_slots, r + 1)
                        for e in range(NE):
                            for b in range(NB):
                                last = pe.matmul(bank[3 + r][:, e:e + 1], slot[:, b, e, :], token[:, b:b + 1],
                                                 start=(b == 0), stop=(b == NB - 1))
                        last.then_inc(R.over_listed, 1)
                    pe.wait_ge(R.over_known, ROUNDS)
                    n = 96 if kind == 0 else 144
                    with pe.Fori(0, ROUNDS) as r:
                        with pe.Fori(0, NE) as e:
                            v = 8 * r + e
                            pe.wait_ge(S.weights, n * v + n)
                            turn_rows(S, v, True)
                            up(S, v, kind, G, lambda j: None)
                            turn_hidden(S, v, kind)
                            if kind == 0:
                                down(S, v, kind, G, dnb_over, lambda j: None, False)
                            else:
                                down1(S, v, G, None, False)

            def down1(S, v, W, arrived, free):
                pe.wait_ge(S.ht_done, v + 1)
                if free:
                    pe.wait_ge(S.y_done, v)
                for kk in range(2):
                    for half in range(2):
                        r = 4 + 2 * kk + half
                        if arrived:
                            arrived(r)
                        for k in range(2):
                            last = pe.matmul(bank[5 + half][:], hT[:, 2 * kk + k, :],
                                             W[:, r * 1024 + k * 512:r * 1024 + (k + 1) * 512],
                                             start=(kk == 0 and k == 0), stop=(kk == 1 and k == 1),
                                             skip_group_check=True)
                        last.then_inc(S.dn_used, 1)

            pe_overflow(R0, O0, 0, 0)

            def arr(g):
                return lambda r: 16 * (CH_L1 // 8 + g + 1)

            pe.wait_ge(xn_ready, 3 * NB)
            transposes(T_LN3, xn)
            pe.wait_ge(t_evicted, T_LN3 + 8)
            layer_N(0, xtok, arr(0), lambda half: None)
            for m in range(KB):
                chunk_T(m, lambda k: xnT[:, k, :], T_Q + m - 1, arr(1)(m), m % 2)
            pe.wait_ge(pe_input, DIAG)
            pe.wait_ge(t_evicted, T_MIX)
            for b in range(NB):
                last = pe.matmul(bank[0][:, b * P:(b + 1) * P], ones, dg[:, b, :], start=True, stop=True)
            last.then_inc(pe_output, 1)
            layer_N(0, xtok, arr(2), lambda half: pe.wait_ge(h_done, 6))
            pe.wait_ge(pe_input, CETS)
            pe.wait_ge(k_done, 6)
            for b in range(NB):
                for db in range(NB):
                    pe.matmul(bank[1][:, b:b + 1], CET[:, db, b * P:(b + 1) * P], ones[:, 0:1],
                              start=(db == 0), stop=(db == NB - 1))
            h = YN(0)
            for b in range(NB):
                for half in range(2):
                    for db in range(NB):
                        last = pe.matmul(bank[2 + 3 * half + b][:], CET[:, db, b * P:(b + 1) * P],
                                         h[:, db, half * 512:(half + 1) * 512], start=(db == 0), stop=(db == NB - 1))
                last.then_inc(agg_ready, 1)
            layer_N(0, xtok, arr(3), lambda half: pe.wait_ge(agg_taken, NB))
            K, V = YN(2), YN(3)
            pe.wait_ge(v_done, 6)
            for a in range(8):
                if a >= 2:
                    pe.wait_ge(kv_taken, a - 1)
                for b in range(NB):
                    pe.matmul(bank[a % 2][:, 0:P], K[:, b, a * P:(a + 1) * P], V[:, b, a * P:(a + 1) * P],
                              start=(b == 0), stop=(b == NB - 1))
                for b in range(NB):
                    last = pe.matmul(bank[a % 2][:, P:P + 2], K[:, b, a * P:(a + 1) * P], ones[:, 0:2],
                                     start=(b == 0), stop=(b == NB - 1))
                last.then_inc(kv_ready, 1)
            for a in range(8):
                pe.wait_ge(kv_taken, 8)
                if a >= 2:
                    pe.wait_ge(num_taken, a - 1)
                for b in range(NB):
                    last = pe.matmul(bank[a % 2][:, b * 130:(b + 1) * 130], YT(1)[:, a, b * P:(b + 1) * P],
                                     kvbd[:, a, :], start=True, stop=True)
                last.then_inc(num_ready, 1)
            pe.wait_ge(num_taken, 8)
            transposes(T_MIX, YN(2))
            pe.wait_ge(t_evicted, T_MIX + 8)
            layer_N(0, tok(1), arr(4), lambda half: None)

            pe.wait_ge(xn_ready, 4 * NB)
            transposes(T_FE, xn)
            pe.wait_ge(t_evicted, T_FE + 8)
            pe.wait_ge(zf_done, 6)
            for b in range(NB):
                for k in range(KB):
                    last = pe.matmul(bank[2][:, b * 8:(b + 1) * 8], xtok(k, b), cent[:, k, :],
                                     start=(k == 0), stop=(k == KB - 1))
            last.then_inc(pe_output, 1)
            route(R1)
            def ring1(e):
                return lambda r: pe.wait_ge(landed[r], 16 * e + 16 * (CH_F1 // 8 + 1))

            pe_experts(M1s, R1, lambda e, b: up(M1s, e, 1, ringf, ring1(e), b),
                       lambda e: down1(M1s, e, ringf, ring1(e), not isinstance(e, int) or e > 0))
            pe_overflow(R1, O1, 1, 1)

        @block.vector
        def _(v):
            step = Chain(v, dstep)
            tt, ts, stt = v.tensor_tensor, v.tensor_scalar, v.scalar_tensor_tensor

            def half_stats(src, b, half):
                return v.bn_stats(st[:, b, 6 * half:6 * half + 6], src[:, b, half * 512:(half + 1) * 512])

            def rstds(c, src, waits=None, halves=(0, 1)):
                for b in range(NB):
                    if waits:
                        waits(b)
                    for half in halves:
                        last = half_stats(src, b, half)
                    step(last)
                    last = v.bn_aggr(mv[:, b, :], st[:, b, :])
                step(last)
                ts(ve[:], mv[:, :, 1], EPS, None, ALU.add).then_inc(var_ready, 1)
                v.wait_ge(var_ready, c + 1)
                v.wait_ge(rstd_seed, c + 1)
                step(tt(nwt[:], rs0[:], rs0[:], ALU.mult))
                step(tt(nwt[:], nwt[:], ve[:], ALU.mult))
                step(ts(nwt[:], nwt[:], -0.5, 1.5, ALU.mult, ALU.add))
                step(tt(rstd[:], rs0[:], nwt[:], ALU.mult))

            def normalise(dst, src, done):
                for b in range(NB):
                    ts(dst[:, b, :], src[:, b, :], mv[:, b, 0:1], rstd[:, b:b + 1],
                       ALU.subtract, ALU.mult).then_inc(done, 1)

            rstds(0, xr, lambda b: v.wait_ge(x_in[b], 16))
            normalise(xn, xr, xn_ready)

            v.memset(zero16[:], 0.0)
            v.wait_ge(edge_in, 16)
            v.tensor_copy(srcf[:], ed[:, 0, :])
            v.tensor_copy(dstf[:], ed[:, 1, :])
            v.tensor_copy(src16[:], ed[:, 0, :])
            v.tensor_copy(dst16[:], ed[:, 1, :])
            step(v.tensor_copy(codef[:], ed[:, 2, :]))
            v.wait_ge(k_in, 48)
            step(stt(keyf[:], srcf[:], float(N), dstf[:], ALU.mult, ALU.add))
            step(ts(wts[:], codef[:], 0.0, 4.0, ALU.is_equal, ALU.mult))
            step(tt(codef[:], codef[:], wts[:], ALU.add))
            stt(codef[:], codef[:], 3.0, digit, ALU.add, ALU.mult).then_inc(edges_ready, 2)
            v.wait_ge(edges_ready, 2)

            v.wait_ge(beta_exp, 2)
            ts(spw[:, 3, :], spw[:, 2, :], 1.0, None, ALU.add).then_inc(act_input, 1)
            step(ts(scale[:, 0:8], scale[:, 0:8], 0.125, None, ALU.mult))
            step(v.tensor_copy(scale[:, 8:16], scale[:, 0:8]))
            v.memset(scale[:, 16:48], 1.0)
            v.memset(scale[:, 48:56], DH ** -0.5)
            step(v.memset(scale[:, 56:64], 1.0))
            tt(sbias[:], cols[:, C_BIAS:C_BIAS + 64], scale[:], ALU.mult).then_inc(cols_ready, 1)
            v.wait_ge(act_input, EW)
            v.wait_ge(act_output, EW)
            step(stt(spw[:, 3, :], spw[:, 3, :], -1.0, spw[:, 2, :], ALU.add, ALU.subtract))
            step(tt(spw[:, 1, :], spw[:, 1, :], spw[:, 3, :], ALU.subtract))
            step(stt(spw[:, 0, :], spw[:, 0, :], 0.0, spw[:, 1, :], ALU.max, ALU.add))

            def dedup(group, q):
                v.wait_ge(keys_ready, group + 1)
                v.wait_ge(edges_ready, group + 2)
                for t in range(GT_):
                    e = group * 8 + t
                    src = bank[4 + 2 * q + t // 4][:, (t % 4) * P:(t % 4 + 1) * P]
                    last = stt(junk[:, t, :], src, keyf[:, bass.ds(e, 1)], later, ALU.is_equal, ALU.mult,
                               accum_out=ndup[:, bass.ds(e, 1)])
                last.then_inc(edges_ready, 1)

            def dedups(layer):
                for q in range(2):
                    dedup(layer * 2 + q, q)

            dedups(0)
            with v.Fori(0, 2) as s:
                step.enter(s, 3)
                v.wait_ge(t_evicted, 8 * s + T_A + 8)
                z = Y[:, bass.ds(s, 1), :].rearrange("p a n -> p (a n)")
                stt(tmp[0], z, -1.0, z, ALU.mult, ALU.min).then_inc(sp_neg, 1)
                dedups(s + 1)
                v.wait_ge(sp_exp, s + 1)
                ts(tmp[0], tmp[1], 1.0, None, ALU.add).then_inc(sp_one, 1)
                v.wait_ge(sp_one, s + 1)
                v.wait_ge(sp_ln, s + 1)
                step(stt(tmp[0], tmp[0], -1.0, tmp[1], ALU.add, ALU.subtract))
                step(tt(tmp[2], tmp[2], tmp[0], ALU.subtract))
                step(stt(z, z, 0.0, tmp[2], ALU.max, ALU.add))
                step.leave(2)
            tt(Y[:, 0, :], Y[:, 0, :], Y[:, 1, :], ALU.mult).then_inc(mixprod, 1)
            with v.Fori(3, 6) as layer:
                dedups(layer)
            v.wait_ge(edges_ready, 2 + EG)
            step(stt(wts[:], ndup[:], 0.0, codef[:], ALU.is_equal, ALU.mult))
            v.wait_ge(mixprod, 1)
            v.memset(M[:], 0.0).then_inc(codes_taken, 3)

            for m in range(KB):
                v.wait_ge(mixs_ready, m + 1)
                s_ = bank[2 + m % 2][:, 0:N]
                r_ = tmp[0][:, m * N:(m + 1) * N]
                step(v.reciprocal(r_, s_))
                step(tt(YT(2)[:, m, :], YT(2)[:, m, :], s_, ALU.mult))
                tt(YT(2)[:, m, :], YT(2)[:, m, :], r_, ALU.mult).then_inc(mixs_taken, 1)

            def onehots(g, q, first=False):
                if not first:
                    v.wait_ge(group_done, g - 1)
                for t in range(GT_):
                    e = g * 8 + t
                    v.tensor_scalar(onehot[:, q, t, 1, :], iota, srcf[:, bass.ds(e, 1)], wts[:, bass.ds(e, 1)],
                                    ALU.is_equal, ALU.mult)
                    v.tensor_scalar(onehot[:, q, t, 0, :], iota, srcf[:, bass.ds(e, 1)], None, ALU.is_equal)
                    v.tensor_scalar(onehot[:, q, t, 2, :], iota, dstf[:, bass.ds(e, 1)], None,
                                    ALU.is_equal).then_inc(oh_ready, 1)

            def take(g, half):
                v.wait_ge(codes_ready, g + 1)
                v.wait_ge(codes_taken, 3 * g + 3)
                for b in range(NB):
                    tt(M[:, half, b, :], bank[2 + b][:, 0:N], M[:, half, b, :], ALU.max).then_inc(codes_taken, 1)

            v.wait_ge(mixs_taken, 8)
            onehots(0, 0, True)
            onehots(1, 1, True)
            take(0, 0)

            def turn_groups(i, half):
                for q in range(2):
                    onehots(2 * i + q, q)
                    take(2 * i + q - 1, half)

            with v.Fori(1, EG // 4) as i:
                turn_groups(i, 0)
            onehots(EG // 2, 0)
            take(EG // 2 - 1, 0)
            onehots(EG // 2 + 1, 1)
            take(EG // 2, 1)
            with v.Fori(EG // 4 + 1, EG // 2) as i:
                turn_groups(i, 1)
            take(EG - 1, 1)

            W9 = NB * N
            code = G[:, 0:W9]
            diag = G[:, W9:2 * W9]
            here = G[:, 2 * W9:3 * W9]
            kind_ = G[:, 3 * W9:4 * W9]
            pick = G[:, 4 * W9:5 * W9]
            mk = mask[:].rearrange("p b n -> p (b n)")
            M1 = Y[:, 1, 0:W9]
            M2 = Y[:, 1, W9:2 * W9]
            v.wait_ge(group_done, EG)
            v.wait_ge(codes_taken, 3 * EG + 3)
            step(stt(code, M2, 0.0, M1, ALU.is_equal, ALU.mult))
            tt(code, code, M2, ALU.add).then_inc(m_taken, 1)
            step(v.memset(diag, 0.0))
            for b in range(NB):
                last = v.tensor_copy(diag[:, b * N + b * P:b * N + (b + 1) * P], ident)
            step(last)
            v.wait_ge(m_taken, 1)
            step(stt(diag, code, 0.0, diag, ALU.is_equal, ALU.mult))
            step(ts(kind_.bitcast(I32), code.bitcast(I32), 21, 3, ALU.logical_shift_right, ALU.bitwise_and))
            step(v.tensor_copy(pick, kind_.bitcast(I32)))
            step(stt(kind_, diag, 3.0, pick, ALU.mult, ALU.add))
            step(stt(here, code, 0.0, diag, ALU.is_gt, ALU.add))
            for c in range(4):
                wc = spw[:, 0, c:c + 1]
                if c == 0:
                    step(ts(mk, kind_, 0.0, wc, ALU.is_equal, ALU.mult))
                else:
                    step(ts(pick, kind_, float(c), wc, ALU.is_equal, ALU.mult))
                    step(tt(mk, mk, pick, ALU.add))
            step(tt(mk, mk, here, ALU.mult))
            step(ts(here, here, -1.0, -NEG, ALU.add, ALU.mult))
            tt(mk, mk, here, ALU.add).then_inc(mask_ready, 1)
            v.wait_ge(mask_ready, 1)

            def read_scores(h, u, ahead):
                for b in range(NB):
                    v.wait_ge(scores_ready, 3 * h + b + 1)
                    if b == 0 and ahead:
                        v.wait_ge(pt_ready, 3 * h - 9)
                    v.memset(tick[:, 3 * u + b:3 * u + b + 1], 0.0)
                    v.tensor_tensor_reduce(out=S[:, u, b, :], in0=bank[2 + b][:, 0:N], in1=mask[:, b, :], scale=-1.0,
                                           scalar=3e38, op0=ALU.add, op1=ALU.min,
                                           accum_out=nmx[:, u, b:b + 1]).then_inc(scores_read, 1)

            def turn_out(h, first=False):
                v.wait_ge(pt_ready, 3 * h + 3)
                if not first:
                    v.wait_ge(av_ready, h)
                v.tensor_copy(PT[:, 2, :], bank[7][:, 0:N]).then_inc(pt2, 1)

            def take_av(h, u):
                v.wait_ge(exp_done, 3 * h + 3)
                step(v.reciprocal(rinv[:, u, :], rsum[:, u, :]))
                v.wait_ge(av_ready, h + 1)
                dst = xn[:, :, bass.ds(h * DH, DH)]
                tt(dst, bank[u % 2][:, 0:NB * DH].rearrange("p (b d) -> p b d", b=NB),
                   rinv[:, u, :].unsqueeze(2).to_broadcast([P, NB, DH]), ALU.mult).then_inc(av_taken, 1)

            v.wait_ge(t_evicted, T_A)
            read_scores(0, 0, False)
            read_scores(1, 1, False)
            for u in range(4):
                turn_out(u, u == 0)
                read_scores(u + 2, (u + 2) % 4, u >= 2)
                take_av(u, u)
            with v.Fori(1, 3) as i:
                step.enter(i - 1, 4)
                for u in range(4):
                    turn_out(4 * i + u)
                    read_scores(4 * i + u + 2, (u + 2) % 4, True)
                    take_av(4 * i + u, u)
                step.leave(2)
            for u in range(4):
                turn_out(12 + u)
                if u < 2:
                    read_scores(14 + u, u + 2, True)
                take_av(12 + u, u)

            v.wait_ge(bias_added, NB)
            for half in range(2):
                v.wait_ge(chunk_used, CH_O + 8 * half + 8)
                for b in range(NB):
                    d = xr[:, b, half * 512:(half + 1) * 512]
                    tt(d, d, bank[2 + 3 * half + b][:], ALU.add).then_inc(x1_done, 1)
                if half == 0:
                    for b in range(NB):
                        v.wait_ge(x1_done, b + 1)
                        half_stats(xr, b, 0)
            rstds(1, xr, lambda b: v.wait_ge(x1_done, 4 + b), (1,))
            v.wait_ge(tp_ready, 16)
            normalise(xn, xr, xn_ready)

            def small(a, n):
                return w[:, a:a + n]
            mx24 = small(400, 72)
            pr = small(200, 192)
            pr4 = pr.rearrange("p (b e j) -> p b e j", b=NB, e=NE)
            pr3 = pr.rearrange("p (b j) -> p b j", j=NE)
            m24 = small(480, 24)
            s24 = small(504, 24)
            l24 = small(528, 24)
            lg = small(24, 24)
            lg3 = lg.rearrange("p (b e) -> p b e", b=NB)
            gat = small(72, 24)
            gat3 = gat.rearrange("p (b e) -> p b e", b=NB)
            m1, m2, i1, dlt = small(3, 3), small(6, 3), small(9, 3), small(0, 3)
            eq = small(96, 24)
            eq3 = eq.rearrange("p (b e) -> p b e", b=NB)
            oh1 = small(120, 24).rearrange("p (b e) -> p b e", b=NB)
            oh2 = small(144, 24).rearrange("p (b e) -> p b e", b=NB)

            def bc(t, n=NE):
                return t.unsqueeze(2).to_broadcast([P, NB, n])

            def first_max(l3, mx, dst, i1=i1):
                step(v.tensor_reduce(mx, l3, AX.X, ALU.max))
                step(tt(eq3, l3, bc(mx), ALU.is_equal))
                step(stt(eq, eq, -100.0, k32[:, 514:538], ALU.mult, ALU.add))
                step(v.tensor_reduce(i1, eq3, AX.X, ALU.min))
                step(ts(i1, i1, 100.0, None, ALU.add))
                step(tt(dst, iota8, bc(i1), ALU.is_equal))

            A3 = small(168, 24).rearrange("p (b e) -> p b e", b=NB)
            rank, posm, posr, rowid = small(600, 24), small(624, 24), small(648, 24), small(672, 24)
            inr, ohk, t24 = small(696, 24), small(720, 24), small(744, 24)
            dest, kept, sc, sco = small(768, 6), small(774, 6), small(780, 6), small(786, 6)
            cmax = small(792, 1)

            def b3(t):
                return t.rearrange("p (b e) -> p b e", b=NB)

            def one_hot_slots(e, where):
                for b in range(NB):
                    last = ts(slot[:, b, e, :], iota[:, 0:CAP], where[:, b * 8 + e:b * 8 + e + 1], None, ALU.is_equal)
                return last

            def route(R):
                v.wait_ge(R.ranked, 1)
                v.tensor_reduce(cmax, bank[2][:, 120:128], AX.X, ALU.max)
                step(v.tensor_copy(rank, bank[2][:, 96:120]))
                step(stt(posm, rank, 1.0, small(168, 24), ALU.add, ALU.mult))
                step(ts(posm, posm, -1.0, None, ALU.add))
                for e in range(NE):
                    one_hot_slots(e, posm).then_inc(R.slots, 1)
                    if e == 0:
                        v.wait_ge(R.listed, 1)
                        v.tensor_copy(idx[:, 0:1], bank[3][:, 0:1]).then_inc(R.rows_known, 1)
                v.wait_ge(R.listed, 2)
                v.tensor_copy(idx[:, 1:8], bank[4][:, 1:8]).then_inc(R.rows_known, 1)
                step(ts(cmax, cmax, float(CAP), None, ALU.is_gt))
                layer = 0 if R is R0 else 1
                v.tensor_copy(flag[:, layer:layer + 1], cmax).then_inc(R.flagged, 1)

            def rows_back(oh, rows_, c, score, out_):
                step(tt(b3(ohk), oh, b3(inr), ALU.mult))
                step(tt(t24, ohk, rows_, ALU.mult))
                step(v.tensor_reduce(kept[:, 3 * c:3 * c + 3], b3(ohk), AX.X, ALU.add))
                step(v.tensor_reduce(dest[:, 3 * c:3 * c + 3], b3(t24), AX.X, ALU.add))
                step(tt(out_[:, 3 * c:3 * c + 3], kept[:, 3 * c:3 * c + 3], score, ALU.mult))

            def scores(R, ohs, ss):
                step(tt(rowid, rank, ebase, ALU.add))
                step(ts(inr, rank, float(CAP), None, ALU.is_lt))
                for c in range(len(ohs)):
                    rows_back(ohs[c], rowid, c, ss[c], sc)
                n = NB * len(ohs)
                v.tensor_copy(idx[:, 8:8 + n], dest[:, 0:n]).then_inc(R.dest_known, 1)

            def v_hidden(S, v_, kind, chain):
                if kind == 0:
                    v.wait_ge(S.sig_done, v_ + 1)
                    chain(tt(hid[:, 0:F0], sg, bank[2][:, 0:F0], ALU.mult))
                    tt(hid[:, 0:F0], hid[:, 0:F0], bank[3][:, 0:F0], ALU.mult).then_inc(S.h_ready, 1)
                    v.wait_ge(S.ht_ready, v_ + 1)
                    v.tensor_copy(hT[:, 0:2, :].rearrange("p f n -> p (f n)"), bank[4][:, 0:2 * P])
                    v.tensor_copy(hT[0:LAST, 2, :], bank[4][0:LAST, 2 * P:3 * P]).then_inc(S.ht_done, 1)
                else:
                    v.wait_ge(S.up_used, 4 * v_ + 4)
                    v.tensor_copy(hid, bank[2][:]).then_inc(S.h_ready, 1)

            def v_output(S, v_, arrived, free):
                v.wait_ge(S.dn_used, 4 * v_ + 4)
                arrived(v_)
                if free:
                    v.wait_ge(S.y_stored, 16 * v_)
                for half in range(2):
                    o = slice(half * 512, (half + 1) * 512)
                    last = tt(Yb[:, o], bank[5 + half][:], b2row[:, o], ALU.add)
                last.then_inc(S.y_done, 1)

            def v_experts(S, kind):
                if kind == 0:
                    with v.Fori(0, NE) as e:
                        step.enter(e, 1)
                        v_hidden(S, e, kind, step)
                        step.leave(NE)
                else:
                    def b2_arrived(e):
                        v.wait_ge(b2_in, 16 * e + 16)

                    v_hidden(S, 0, kind, step)
                    v_hidden(S, 1, kind, step)
                    v_output(S, 0, b2_arrived, False)
                    with v.Fori(2, NE) as e:
                        v_hidden(S, e, kind, step)
                        v_output(S, e - 1, b2_arrived, True)
                    v_output(S, NE - 1, b2_arrived, True)

            def v_overflow(R, S, kind, layer, choices):
                over = v.value_load(flag[0:1, layer:layer + 1])
                chain = Chain(v, ostep[layer])
                ohs, ss = [oh1, oh2][:choices], [m1, m2][:choices]
                with v.If(over > 0):
                    for r in range(ROUNDS):
                        if r:
                            v.wait_ge(R.over_listed, r)
                        chain(ts(posr, posm, -float(CAP * (r + 1)), None, ALU.add))
                        for e in range(NE):
                            last = one_hot_slots(e, posr)
                        last.then_inc(R.over_slots, 1)
                        v.wait_ge(R.over_listed, r + 1)
                        v.tensor_copy(idx[:, 16 + 8 * r:24 + 8 * r], bank[3 + r][:, 0:8]).then_inc(R.over_known, 1)
                    chain(ts(posr, rank, 2.0 * CAP, float((NE - 1) * CAP), ALU.is_ge, ALU.mult))
                    chain(stt(rowid, rowid, -float(CAP), posr, ALU.add, ALU.add))
                    chain(ts(inr, rank, float(CAP), None, ALU.is_ge))
                    for c in range(choices):
                        chain(tt(b3(ohk), ohs[c], b3(inr), ALU.mult))
                        chain(tt(t24, ohk, rowid, ALU.mult))
                        chain(v.tensor_reduce(kept[:, 3 * c:3 * c + 3], b3(ohk), AX.X, ALU.add))
                        chain(v.tensor_reduce(dest[:, 3 * c:3 * c + 3], b3(t24), AX.X, ALU.add))
                        chain(tt(sco[:, 3 * c:3 * c + 3], kept[:, 3 * c:3 * c + 3], ss[c], ALU.mult))
                    n = NB * choices
                    v.tensor_copy(idx[:, 32:32 + n], dest[:, 0:n]).then_inc(R.over_known, 1)
                    v.memset(tick[:, 0:1], 0.0).then_inc(S.turn, 1)
                    with v.Fori(0, ROUNDS) as r:
                        with v.Fori(0, NE) as e:
                            t = 8 * r + e
                            if kind == 0:
                                chain.enter(t, 1)
                            v_hidden(S, t, kind, chain)
                            if kind == 1:
                                v_output(S, t, lambda e_: v.wait_ge(S.weights, 144 * e_ + 144), False)
                            v.wait_ge(S.y_stored, 16 * t + 16)
                            v.wait_ge(S.turn, t + 1)
                            v.memset(tick[:, 0:1], 0.0).then_inc(S.turn, 1)
                            if kind == 0:
                                chain.leave(ROUNDS * NE)
                    for m in range(n):
                        b = m % NB
                        v.wait_ge(S.back, 16 * m + 16)
                        v.wait_ge(S.turn, ROUNDS * NE + m + 1)
                        stt(xr[:, b, :], Xg, sco[:, m:m + 1], xr[:, b, :], ALU.mult, ALU.add).then_inc(S.turn, 1)
                    v.wait_ge(S.turn, ROUNDS * NE + n + 1)

            v.wait_ge(pe_output, MIXED)
            step(v.tensor_copy(mx24, bank[2][:, 0:72]))
            mixed = mx24.rearrange("p (b c) -> p b c", b=NB)
            for b in range(NB):
                last = tt(pr4[:, b], mixed[:, b, 0:8].unsqueeze(2).to_broadcast([P, NE, NE]),
                          mixed[:, b, 8:16].unsqueeze(1).to_broadcast([P, NE, NE]), ALU.mult)
            step(last)
            step(v.tensor_reduce(m24, pr3, AX.X, ALU.max))
            tt(pr3, pr3, m24.unsqueeze(2).to_broadcast([P, 24, NE]), ALU.subtract).then_inc(act_input, 1)
            v.wait_ge(act_output, GL)
            step(v.tensor_reduce(s24, pr3, AX.X, ALU.add))
            for b in range(NB):
                last = tt(pr4[:, b], pr4[:, b], mixed[:, b, 16:24].unsqueeze(1).to_broadcast([P, NE, NE]), ALU.mult)
            step(last)
            step(v.tensor_reduce(l24, pr3, AX.X, ALU.add))
            step(v.reciprocal(s24, s24))
            step(tt(lg, l24, s24, ALU.mult))
            first_max(lg3, m1, oh1)
            step(stt(lg3, oh1, -3e38, lg3, ALU.mult, ALU.add))
            first_max(lg3, m2, oh2)
            tt(A3, oh1, oh2, ALU.add).then_inc(R0.assigned, 1)
            tt(dlt, m2, m1, ALU.subtract).then_inc(act_input, 1)
            route(R0)
            v.wait_ge(act_output, G2)
            step(ts(m1, dlt, 1.0, None, ALU.add))
            step(v.reciprocal(m1, m1))
            step(tt(m2, dlt, m1, ALU.mult))
            scores(R0, [oh1, oh2], [m1, m2])
            v_experts(M0, 0)
            v_overflow(R0, O0, 0, 0, 2)
            for b in range(NB):
                v.wait_ge(back_in[b], 32)
                for c in range(2):
                    ins = stt(xr[:, b, :], back[:, c * NB + b, :], sc[:, c * NB + b:c * NB + b + 1], xr[:, b, :],
                              ALU.mult, ALU.add)
                    if c == 0:
                        step(ins)
                ins.then_inc(x2_done, 1)
            rstds(2, xr, lambda b: v.wait_ge(x2_done, 1 + b))
            normalise(xn, xr, xn_ready)

            v.wait_ge(l1_in, 16)
            v.wait_ge(h_done, 6)
            h = YN(0)
            for b in range(NB):
                step(v.tensor_tensor_reduce(out=prod, in0=h[:, b, :], in1=a_l, scale=1.0, scalar=0.0,
                                            op0=ALU.mult, op1=ALU.add, accum_out=al[:, b:b + 1]))
                step(v.tensor_tensor_reduce(out=prod, in0=h[:, b, :], in1=a_r, scale=1.0, scalar=0.0,
                                            op0=ALU.mult, op1=ALU.add, accum_out=ar[:, b:b + 1]))
            for b in range(NB):
                last = ts(dg[:, b, :], ident, al[:, b:b + 1], None, ALU.mult)
            last.then_inc(pe_input, 1)
            v.wait_ge(pe_output, ALBC)
            for b in range(NB):
                last = ts(CET[:, b, :], bank[0][:, 0:N], ar[:, b:b + 1], -1.0, ALU.add, ALU.mult)
            step(last)
            stt(eT[:], CET[:], 0.1, CET[:], ALU.mult, ALU.min).then_inc(act_input, 1)
            v.wait_ge(act_output, ZE)
            tt(CET[:], CT[:], eT[:], ALU.mult).then_inc(pe_input, 1)
            v.wait_ge(rows2_in, 32)
            for b in range(NB):
                last = tt(xr[:, b, :], xr[:, b, :], rows[:, 1, :], ALU.add)
            step(last)
            v.wait_ge(agg_ready, 1)
            step(ts(rsm, bank[1][:, 0:NB], 1e-5, None, ALU.add))
            step(v.reciprocal(rsi, rsm))
            t_ = YN(4)
            for b in range(NB):
                v.wait_ge(agg_ready, b + 1)
                ts(t_[:, b, 0:512], bank[2 + b][:], rsi[:, b:b + 1], None, ALU.mult)
                ts(t_[:, b, 512:1024], bank[5 + b][:], rsi[:, b:b + 1], None, ALU.mult).then_inc(agg_taken, 1)
            v.wait_ge(agg_taken, NB)
            ts(Y[:, 5, :], Y[:, 4, :], 0.0, None, ALU.min).then_inc(act_input, 1)
            v.wait_ge(act_output, EL)
            xf = xr[:].rearrange("p b d -> p (b d)")
            step(stt(xf, Y[:, 4, :], 0.0, xf, ALU.max, ALU.add))
            step(stt(xf, Y[:, 5, :], -1.0, xf, ALU.add, ALU.add))

            for a in range(8):
                v.wait_ge(kv_ready, a + 1)
                tt(kvbd[:, a, :], bank[a % 2][:, 0:130], bdx, ALU.mult).then_inc(kv_taken, 1)
            for a in range(8):
                v.wait_ge(num_ready, a + 1)
                if a:
                    v.wait_ge(num_taken, a)
                nd = bank[a % 2][:, 0:390].rearrange("p (b c) -> p b c", b=NB)
                step(ts(den[:], nd[:, :, 128:130], 1e-8, None, ALU.add))
                step(v.reciprocal(rden[:], den[:]))
                for j in range(2):
                    last = tt(YN(2)[:, :, a * P + j * DH:a * P + (j + 1) * DH], nd[:, :, j * DH:(j + 1) * DH],
                              rden[:, :, j:j + 1].to_broadcast([P, NB, DH]), ALU.mult)
                last.then_inc(num_taken, 1)
            for half in range(2):
                v.wait_ge(chunk_used, CH_L1 + 32 + 4 * half + 4)
                for b in range(NB):
                    sl = slice(half * 512, (half + 1) * 512)
                    tt(YN(3)[:, b, sl], bank[2 + 3 * half + b][:], xn[:, b, sl], ALU.add).then_inc(zf_done, 1)
                if half == 0:
                    for b in range(NB):
                        v.wait_ge(zf_done, b + 1)
                        half_stats(YN(3), b, 0)
            rstds(3, YN(3), lambda b: v.wait_ge(zf_done, 4 + b), (1,))
            z3 = YN(3)
            for b in range(NB):
                step(stt(z3[:, b, :], z3[:, b, :], mv[:, b, 0:1], rows[:, 0, :], ALU.subtract, ALU.mult))
                step(stt(xr[:, b, :], z3[:, b, :], rstd[:, b:b + 1], xr[:, b, :], ALU.mult, ALU.add))
            rstds(4, xr)
            normalise(xn, xr, xn_ready)

            v.wait_ge(xn_ready, 4 * NB)
            rstds(5, xn)
            normalise(YN(2), xn, xh_ready)
            v.wait_ge(pe_output, AFF)
            v.tensor_copy(small(216, 24), bank[2][:, 0:24]).then_inc(act_input, 1)
            v.wait_ge(act_input, AF)
            aff = small(216, 24).rearrange("p (b e) -> p b e", b=NB)
            first_max(aff, small(204, 3), oh1)
            v.tensor_copy(A3, oh1).then_inc(R1.assigned, 1)
            route(R1)
            v.wait_ge(act_output, AF)
            step(tt(gat, small(120, 24), small(24, 24), ALU.mult))
            step(v.tensor_reduce(m1, gat3, AX.X, ALU.add))
            scores(R1, [oh1], [m1])
            v_experts(M1s, 1)
            v.wait_ge(feats_added, NB)
            v_overflow(R1, O1, 1, 1, 1)
            for b in range(NB):
                v.wait_ge(back_in[b], 48)
                stt(xr[:, b, :], back[:, b, :], sc[:, b:b + 1], xr[:, b, :], ALU.mult, ALU.add).then_inc(y_ready, 1)


def t_chunks(a):
    m = a.shape[1] // P
    return np.ascontiguousarray(a.reshape(KB, P, m, P).transpose(2, 1, 0, 3)).reshape(m, P, 1024)


def n_chunks(a):
    k = a.shape[0] // 256
    return np.ascontiguousarray(a.reshape(k, 2, P, 2, 512).transpose(0, 3, 2, 1, 4)).reshape(k, 2, P, 1024)


def halves(*mats):
    cs = [n_chunks(a) for a in mats]
    return [c[:, h] for h in range(2) for c in cs]


def weight_stream(I):
    parts = [t_chunks(I[n].T) for n in ("L0_mix_Wq", "L0_mix_Wk", "L0_mix_Wv", "L0_gnn_wq", "L0_gnn_wk", "L0_gnn_wv",
                                        "L0_gnn_wiq", "L0_gnn_wik")]
    parts += halves(I["L0_gnn_wiv"].T)
    parts += halves(I["L0_mix_Wo"].T, I["L0_gnn_wo"].T)
    parts += halves(I["L1_gnn_W"])
    parts += [t_chunks(I["L1_mix_W_Q"])]
    parts += halves(I["L1_mix_W_K"]) + halves(I["L1_mix_W_V"]) + halves(I["L1_mix_W_fc"])
    for e in range(NE):
        w1 = I["L1_ffn_w1"][e].reshape(4, 2, P, F1).transpose(0, 2, 1, 3).reshape(4, P, 1024)
        parts += [w1, n_chunks(I["L1_ffn_w2"][e]).reshape(4, P, 1024)]
    stream = np.concatenate(parts)
    assert stream.shape[0] == CHUNKS
    return stream


def constants():
    f = np.float32
    part, col = np.arange(P)[:, None], np.arange(P)[None, :]
    ident = (part == col).astype(f)
    bd = (part // DH == col // DH).astype(f)
    headcol = (part // DH == np.arange(2)[None, :]).astype(f)
    later = (col > part).astype(f)
    iota8 = np.tile(np.arange(NE, dtype=f) + 100, (P, NB))
    digit = np.tile(np.ldexp(f(1), 3 * (np.arange(ET) % 48) - 72).astype(f), (P, 1))
    ebase = np.tile(np.arange(NE, dtype=f) * CAP, (P, NB))
    c32 = np.concatenate([ident, bd, headcol, later, np.ones((P, P), f), iota8, digit, ebase], 1)
    token = np.arange(N).reshape(NB, P).T
    c16 = np.concatenate([np.tile(np.arange(N), (P, 1)), ident, ident * N, token], 1).astype(np.float16)
    return c32, c16


def kernel(**inputs):
    import concourse.bacc as bacc
    from concourse.bass_utils import run_bass_kernel_spmd as run

    I = {k: np.asarray(a) for k, a in inputs.items()}
    c32, c16 = constants()

    def col(a, m=KB):
        return a.reshape(m, P).T

    cols = np.concatenate(
        [col(I[n]) for n in ("L0_mix_bq", "L0_mix_bk", "L0_mix_bv", "L0_gnn_bq", "L0_gnn_bk", "L0_gnn_bv",
                             "L0_gnn_biq", "L0_gnn_bik", "L0_gnn_biv")]
        + [col(np.repeat(I["L0_mix_beta"], DH)), col(I["L1_ffn_b1"], 32), col(I["L1_ffn_gamma"], 64),
           col(I["L1_ffn_beta"], 64), np.tile(I["L0_gnn_edge_type_weights"], (P, 1))], 1)
    edges = np.stack([I[n].reshape(ET, P).T for n in ("src", "dst", "edge_type_5")], 1)
    arrays = {
        "x": I["x"], "stream": weight_stream(I), "c32": c32, "c16": c16, "cols": cols, "edges": edges,
        "up0": I["L0_ffn_w1"].transpose(0, 2, 1).reshape(NE, 4, 2, P, 2 * F0).transpose(0, 1, 3, 2, 4)
        .reshape(NE, 4, P, UPW),
        "dn0": I["L0_ffn_w2"].transpose(0, 2, 1),
        "wqkv": I["L0_ffn_wqkv"].T.reshape(KB, P, 3 * NE).transpose(1, 0, 2),
        "cent": I["L1_ffn_centroids"].T.reshape(KB, P, NE).transpose(1, 0, 2),
        "bo_g": I["L0_gnn_bo"].reshape(1, D), "bo_m": I["L0_mix_bo"].reshape(1, D),
        "a_lr": I["L1_gnn_a"], "gamma": I["L1_mix_gamma"].reshape(1, D), "beta": I["L1_mix_beta"].reshape(1, D),
        "b2": I["L1_ffn_b2"].reshape(NE, 1, D),
    }
    arrays = {k: np.ascontiguousarray(a) for k, a in arrays.items()}
    nc = bacc.Bacc("TRN2", target_bir_lowering=False, num_devices=1)
    args = [nc.dram_tensor("in_" + k, a.shape, mybir.dt.from_np(a.dtype), kind="ExternalInput").ap()
            for k, a in arrays.items()]
    for name, n in (("xs", N), ("ys", NE * CAP), ("yo", ROUNDS * NE * CAP)):
        args.append(nc.dram_tensor(name, (n, D), F32, kind="Internal").ap())
    out = nc.dram_tensor("out", (N, D), F32, kind="ExternalOutput").ap()
    program(nc, *args, out)
    r = run(nc, [{"in_" + k: a for k, a in arrays.items()}], core_ids=[0])
    return r.results[0]["out"]
```
